# Optimizing a Trainium2 kernel written in Bass

```python
import numpy as np
import jax
import jax.numpy as jnp

def _softmax(x, axis=-1):
    return jax.nn.softmax(x, axis=axis)

def _gelu(x):
    return jax.nn.gelu(x, approximate=True)

def _silu(x):
    return jax.nn.silu(x)

def _sigmoid(x):
    return jax.nn.sigmoid(x)

def _layernorm(x, axis=-1, eps=1e-05):
    m = jnp.mean(x, axis=axis, keepdims=True)
    v = jnp.var(x, axis=axis, keepdims=True)
    return (x - m) / jnp.sqrt(v + eps)

def _scatter_add(tgt, idx, src, axis=0):
    return tgt.at[idx].add(src)

def _segment_sum(src, seg, n):
    return jax.ops.segment_sum(src, seg, n)
kernel_name = 'mk_xattn_ffn_d1_seqx_r8_f7d8eb'

def setup_inputs(seed: int=0):
    np.random.seed(seed)
    _w = jnp.asarray

    def _rec_inputs():
        import jax
        import jax.numpy as jnp
        _rk = jax.random.key(seed)
        x = 4.136e-05 + 0.9999 * jax.random.normal(jax.random.fold_in(_rk, 1), (32, 56, 128), jnp.float32)
        _lenS = 56 - jax.random.randint(jax.random.fold_in(_rk, 7), (32,), 0, max(1, 56 // 4) + 1, jnp.int32)
        _lenS2 = 1500 - jax.random.randint(jax.random.fold_in(_rk, 8), (32,), 0, max(1, 1500 // 4) + 1, jnp.int32)
        _ctx_1024P = jax.random.normal(jax.random.fold_in(_rk, 11), (32, 16, 128), jnp.float32)
        _ctx_1024c = jax.random.dirichlet(jax.random.fold_in(_rk, 511), 0.3 * jnp.ones((16,), jnp.float32), (32, 1500))
        _ctx_1024t = jnp.einsum('bsk,bkd->bsd', _ctx_1024c, _ctx_1024P)
        _ctx_1024t = _ctx_1024t * jax.lax.rsqrt(jnp.mean(jnp.square(_ctx_1024t)) + 1e-12) * 0.953939
        ctx_1024 = 7.22013e-05 + 1.00017 * (_ctx_1024t + 0.3 * jax.random.normal(jax.random.fold_in(_rk, 611), (32, 1500, 128), jnp.float32))
        _validS = jnp.arange(56)[None, :] < _lenS[:, None]
        _validS2 = jnp.arange(1500)[None, :] < _lenS2[:, None]
        _causal = jnp.tril(jnp.ones((56, 56), dtype=bool))
        mask_BxSxS2_bf1 = jnp.ones((32, 56, 1500), dtype=bool)
        return (x, ctx_1024, mask_BxSxS2_bf1)
    x, ctx_1024, mask_BxSxS2_bf1 = _rec_inputs()

    def _L0_xattn_setup():
        import jax, jax.numpy as jnp
        import numpy as np
        B, T, C, H = (4, 256, 128, 16)
        HD = C // H
        key = jax.random.key(seed)
        ks = jax.random.split(key, 8)
        s = 0.02
        return {'k': jax.random.normal(ks[0], (B, T, C), jnp.float32), 'q': jax.random.normal(ks[1], (B, T, C), jnp.float32), 'v': jax.random.normal(ks[2], (B, T, C), jnp.float32), 'mask': jnp.ones((B, T, T), dtype=bool), 'Wk': jax.random.normal(ks[3], (C, C), jnp.float32) * s, 'bk': jnp.zeros((C,), jnp.float32), 'Wq': jax.random.normal(ks[4], (C, C), jnp.float32) * s, 'bq': jnp.zeros((C,), jnp.float32), 'Wv': jax.random.normal(ks[5], (C, C), jnp.float32) * s, 'bv': jnp.zeros((C,), jnp.float32), 'Wo': jax.random.normal(ks[6], (C, C), jnp.float32) * s, 'bo': jnp.zeros((C,), jnp.float32)}
    _L0_xattn_all = _L0_xattn_setup()
    _L0_xattn_in = {k: v for k, v in _L0_xattn_all.items() if k in ('Wk', 'bk', 'Wq', 'bq', 'Wv', 'bv', 'Wo', 'bo')}
    del _L0_xattn_all

    def _L0_ffn_setup():
        import jax, jax.numpy as jnp
        import numpy as np
        D_MODEL = 128
        FF = 512
        E = 8
        TOP_K = 2
        CAP_FACTOR = 1.25
        B, T = (4, 256)

        def _moe_forward(x, gate_w, gate_b, w1, b1, w2, b2):
            Bb, Tt, d = x.shape
            S = Bb * Tt
            C = int(CAP_FACTOR * S / E)
            xf = x.reshape(S, d)
            logits = xf @ gate_w + gate_b
            probs = jax.nn.softmax(logits, axis=1)
            topk_p, topk_i = jax.lax.top_k(probs, TOP_K)
            topk_pn = topk_p / jnp.sum(topk_p, axis=1, keepdims=True)
            rows = jnp.arange(S)
            w_te = jnp.zeros((S, E), xf.dtype).at[rows[:, None], topk_i].set(topk_pn)
            mask = jnp.zeros((S, E), bool).at[rows[:, None], topk_i].set(True)
            rank = jnp.cumsum(mask.astype(jnp.int32), axis=0)
            slot = jnp.where(mask & (rank <= C), rank - 1, C)
            e_grid = jnp.broadcast_to(jnp.arange(E), (S, E))
            t_grid = jnp.broadcast_to(rows[:, None], (S, E))
            buf = jnp.full((E, C + 1), S, jnp.int32).at[e_grid, slot].set(t_grid)
            idx = buf[:, :C]
            valid = idx < S
            x_pad = jnp.concatenate([xf, jnp.zeros((1, d), xf.dtype)], axis=0)
            xin = x_pad[idx]
            h = jax.nn.relu(jnp.einsum('ecd,edh->ech', xin, w1) + b1[:, None, :])
            out = jnp.einsum('ech,ehd->ecd', h, w2) + b2[:, None, :]
            w_pad = jnp.concatenate([w_te, jnp.zeros((1, E), xf.dtype)], axis=0)
            tok_w = w_pad[idx, jnp.arange(E)[:, None]]
            out = out * jnp.where(valid, tok_w, 0.0)[:, :, None]
            final = jnp.zeros((S + 1, d), xf.dtype).at[idx.reshape(-1)].add(out.reshape(-1, d))[:S]
            return final.reshape(Bb, Tt, d)
        key = jax.random.key(seed)
        ks = jax.random.split(key, 7)
        s = 0.02
        return {'x': jax.random.normal(ks[0], (B, T, D_MODEL), jnp.float32), 'gate_w': jax.random.normal(ks[1], (D_MODEL, E), jnp.float32) * s, 'gate_b': jnp.zeros((E,), jnp.float32), 'w1': jax.random.normal(ks[2], (E, D_MODEL, FF), jnp.float32) * s, 'b1': jnp.zeros((E, FF), jnp.float32), 'w2': jax.random.normal(ks[3], (E, FF, D_MODEL), jnp.float32) * s, 'b2': jnp.zeros((E, D_MODEL), jnp.float32)}
    _L0_ffn_all = _L0_ffn_setup()
    _L0_ffn_in = {k: v for k, v in _L0_ffn_all.items() if k in ('gate_w', 'gate_b', 'w1', 'b1', 'w2', 'b2')}
    del _L0_ffn_all
    return {'x': x, 'ctx_1024': ctx_1024, 'mask_BxSxS2_bf1': mask_BxSxS2_bf1, 'L0_xattn_Wk': _L0_xattn_in['Wk'], 'L0_xattn_bk': _L0_xattn_in['bk'], 'L0_xattn_Wq': _L0_xattn_in['Wq'], 'L0_xattn_bq': _L0_xattn_in['bq'], 'L0_xattn_Wv': _L0_xattn_in['Wv'], 'L0_xattn_bv': _L0_xattn_in['bv'], 'L0_xattn_Wo': _L0_xattn_in['Wo'], 'L0_xattn_bo': _L0_xattn_in['bo'], 'L0_ffn_gate_w': _L0_ffn_in['gate_w'], 'L0_ffn_gate_b': _L0_ffn_in['gate_b'], 'L0_ffn_w1': _L0_ffn_in['w1'], 'L0_ffn_b1': _L0_ffn_in['b1'], 'L0_ffn_w2': _L0_ffn_in['w2'], 'L0_ffn_b2': _L0_ffn_in['b2']}

def reference(x, ctx_1024, mask_BxSxS2_bf1, L0_xattn_Wk, L0_xattn_bk, L0_xattn_Wq, L0_xattn_bq, L0_xattn_Wv, L0_xattn_bv, L0_xattn_Wo, L0_xattn_bo, L0_ffn_gate_w, L0_ffn_gate_b, L0_ffn_w1, L0_ffn_b1, L0_ffn_w2, L0_ffn_b2):
    import jax
    import jax.numpy as jnp

    def _L0_xattn_ref(k, q, v, mask, Wk, bk, Wq, bq, Wv, bv, Wo, bo):
        import jax, jax.numpy as jnp
        import numpy as np
        B, T, C, H = (4, 256, 128, 16)
        HD = C // H
        Bn, Tk, Cn = k.shape
        Tq = q.shape[1]
        hd = Cn // H
        kp = (k @ Wk + bk).reshape(Bn, Tk, H, hd).transpose(0, 2, 1, 3)
        qp = (q @ Wq + bq).reshape(Bn, Tq, H, hd).transpose(0, 2, 1, 3)
        vp = (v @ Wv + bv).reshape(Bn, Tk, H, hd).transpose(0, 2, 1, 3)
        att = jnp.einsum('bhqd,bhkd->bhqk', qp, kp) * (1.0 / jnp.sqrt(jnp.float32(hd)))
        causal = jnp.tril(jnp.ones((Tq, Tk), dtype=bool))
        m = causal[None, None, :, :] & mask[:, None, :, :]
        att = jnp.where(m, att, jnp.float32(-1000000000.0))
        att = jax.nn.softmax(att, axis=-1)
        y = jnp.einsum('bhqk,bhkd->bhqd', att, vp)
        y = y.transpose(0, 2, 1, 3).reshape(Bn, Tq, Cn)
        return y @ Wo + bo

    def _L0_ffn_ref(x, gate_w, gate_b, w1, b1, w2, b2):
        import jax, jax.numpy as jnp
        import numpy as np
        D_MODEL = 128
        FF = 512
        E = 8
        TOP_K = 2
        CAP_FACTOR = 1.25
        B, T = (4, 256)

        def _moe_forward(x, gate_w, gate_b, w1, b1, w2, b2):
            Bb, Tt, d = x.shape
            S = Bb * Tt
            C = int(CAP_FACTOR * S / E)
            xf = x.reshape(S, d)
            logits = xf @ gate_w + gate_b
            probs = jax.nn.softmax(logits, axis=1)
            topk_p, topk_i = jax.lax.top_k(probs, TOP_K)
            topk_pn = topk_p / jnp.sum(topk_p, axis=1, keepdims=True)
            rows = jnp.arange(S)
            w_te = jnp.zeros((S, E), xf.dtype).at[rows[:, None], topk_i].set(topk_pn)
            mask = jnp.zeros((S, E), bool).at[rows[:, None], topk_i].set(True)
            rank = jnp.cumsum(mask.astype(jnp.int32), axis=0)
            slot = jnp.where(mask & (rank <= C), rank - 1, C)
            e_grid = jnp.broadcast_to(jnp.arange(E), (S, E))
            t_grid = jnp.broadcast_to(rows[:, None], (S, E))
            buf = jnp.full((E, C + 1), S, jnp.int32).at[e_grid, slot].set(t_grid)
            idx = buf[:, :C]
            valid = idx < S
            x_pad = jnp.concatenate([xf, jnp.zeros((1, d), xf.dtype)], axis=0)
            xin = x_pad[idx]
            h = jax.nn.relu(jnp.einsum('ecd,edh->ech', xin, w1) + b1[:, None, :])
            out = jnp.einsum('ech,ehd->ecd', h, w2) + b2[:, None, :]
            w_pad = jnp.concatenate([w_te, jnp.zeros((1, E), xf.dtype)], axis=0)
            tok_w = w_pad[idx, jnp.arange(E)[:, None]]
            out = out * jnp.where(valid, tok_w, 0.0)[:, :, None]
            final = jnp.zeros((S + 1, d), xf.dtype).at[idx.reshape(-1)].add(out.reshape(-1, d))[:S]
            return final.reshape(Bb, Tt, d)
        return _moe_forward(x, gate_w, gate_b, w1, b1, w2, b2)
    x = x + _L0_xattn_ref(ctx_1024, _layernorm(x, axis=-1), ctx_1024, mask_BxSxS2_bf1, L0_xattn_Wk, L0_xattn_bk, L0_xattn_Wq, L0_xattn_bq, L0_xattn_Wv, L0_xattn_bv, L0_xattn_Wo, L0_xattn_bo)
    x = x + _L0_ffn_ref(_layernorm(x, axis=-1), L0_ffn_gate_w, L0_ffn_gate_b, L0_ffn_w1, L0_ffn_b1, L0_ffn_w2, L0_ffn_b2)
    return x

_drawn_inputs = setup_inputs


def setup_inputs(seed=0):
    import zlib

    import numpy as np

    out = dict(_drawn_inputs(seed))
    spreads = {'L0_xattn_bk': (0.0, 2.0),
     'L0_xattn_bq': (0.0, 2.0),
     'L0_xattn_bv': (0.0, 0.308),
     'L0_xattn_bo': (0.0, 0.1),
     'L0_ffn_gate_b': (0.0, 0.1),
     'L0_ffn_b1': (0.0, 0.495),
     'L0_ffn_b2': (0.0, 0.1)}
    factors = {'L0_xattn_Wk': 8.0, 'L0_xattn_Wq': 8.0}
    for name, (base, spread) in spreads.items():
        noise = np.random.default_rng([zlib.crc32(name.encode()), seed]).standard_normal(out[name].shape)
        drawn = base * np.exp(spread * noise) if base else spread * noise
        out[name] = jnp.asarray(drawn.astype(out[name].dtype))
    for name, factor in factors.items():
        out[name] = (out[name] * factor).astype(out[name].dtype)
    return out
```

```python
from contextlib import ExitStack

import numpy as np

import concourse.bass as bass
from concourse import mybir

B, S, S2, D = 32, 56, 1500, 128
H, HD = 16, 8
E, FF, TOP_K = 8, 512, 2
CAP = int(1.25 * B * S / E)
SLOT_TILE = 96
SLOT_TILES = 3
SLOTS = SLOT_TILE * SLOT_TILES
PAD = 64
PAIRS = B // 2
GP = 2
GROUPS = PAIRS // GP
GT = GP * 2 * PAD
KEYS = S + 1
HP = H // 2
VW = 2 * (HD + 1)
FC = FF // 128
REC = D + 2
N_DST = TOP_K * B * S
FAR = 8192.0
GONE = -1.0e30
Q_RUNS = [(0, 0, 3), (3, 0, 2), (5, 0, 1)]
K_RUNS = [(0, 0, 1), (1, 0, 1), (2, 0, 1), (3, 1, 1), (4, 1, 1), (5, 2, 1)]
SLOT6 = 6 * HD
N_STACK = len(Q_RUNS) + len(K_RUNS)
KQ = 4
KCH = 25
N_KCH = S2 // KQ // KCH


def wait(eng, sem, value):
    if isinstance(value, int) and value <= 0:
        return
    eng.wait_ge(sem, value)


def hold(eng, passed):
    eng.sem_inc(passed, 1)


def build(nc, x, ctx, mask, wk, bk, wq, bq, wv, bv, wo, bo, gate_w, gate_b, w1, b1, w2, b2, out):
    f32, bf16, i32, u8 = mybir.dt.float32, mybir.dt.bfloat16, mybir.dt.int32, mybir.dt.uint8
    ALU, ACT, X = mybir.AluOpType, mybir.ActivationFunctionType, mybir.AxisListType.X
    add, sub, mult = ALU.add, ALU.subtract, ALU.mult

    with ExitStack() as stack:
        def sb(name, shape, dt=f32):
            return stack.enter_context(nc.sbuf_tensor(name, shape, dt))

        def sem(name):
            return stack.enter_context(nc.semaphore(name))

        def dram(name, shape, dt=f32):
            return nc.dram_tensor(name, shape, dt, kind="Internal").ap()

        parts_d = dram("parts_d", (GROUPS, 2, 3, D, GT), bf16)
        slots_d = dram("slots_d", (E * SLOTS, REC))
        choice_d = dram("choice_d", (N_DST, D))
        sums_d = dram("sums_d", (KQ * B, D))
        mean_d = dram("mean_d", (B, D))

        ident = sb("ident", [128, 128])
        ident_b = sb("ident_b", [128, 128], bf16)
        causal = sb("causal", [128, S], bf16)
        before = sb("before", [128, 128], bf16)
        valid = sb("valid", [128, 128], bf16)
        slot_base_i = sb("slot_base_i", [128, E], i32)
        slot_base = sb("slot_base", [128, E])
        order_i = sb("order_i", [128, E], i32)
        order = sb("order", [128, E])
        dest_i = sb("dest_i", [128, TOP_K, PAIRS], i32)
        dest = sb("dest", [128, TOP_K, PAIRS])
        row_ok, row_far = sb("row_ok", [128, 1]), sb("row_far", [128, 1])
        minus_half = sb("minus_half", [128, GP])
        wq_s, wk_s, wv_s, wo_s = (sb(n, [128, D]) for n in ("wq_s", "wk_s", "wv_s", "wo_s"))
        bq_s, bk_s, bqs = (sb(n, [128, 1]) for n in ("bq_s", "bk_s", "bqs"))
        bv_s, bo_s = sb("bv_s", [128, D]), sb("bo_s", [128, D])
        gw_s, gb_s = sb("gw_s", [128, E]), sb("gb_s", [128, E])
        b1_s = sb("b1_s", [128, E, FC])
        b2_s = sb("b2_s", [128, E, D])
        xs = sb("xs", [128, PAIRS, D])
        x2 = sb("x2", [128, PAIRS, D])
        m8 = sb("m8", [128, PAIRS, S], u8)
        mc = sb("mc", [128, PAIRS, S], bf16)
        some = sb("some", [128, PAIRS], bf16)
        bias = sb("bias", [128, PAIRS, PAD], bf16)
        rows_kept = sb("rows_kept", [1, 1])
        all_gone = sb("all_gone", [1, 1], i32)

        key_sum = sb("key_sum", [128, D])
        keys_c = sb("keys_c", [128, KCH, D])
        quarter = sb("quarter", [B, KQ, D])
        mean = sb("mean", [B, D])

        ctxk = sb("ctxk", [128, GP, D])
        ctxv = sb("ctxv", [128, GP, D])
        stat1, mv1 = sb("stat1", [128, GP, 6]), sb("mv1", [128, GP, 2])
        ve1, rs1 = sb("ve1", [128, GP]), sb("rs1", [128, GP])
        xn = sb("xn", [128, GP, D])
        frontT = sb("frontT", [128, 2, GT])
        qk = sb("qk", [128, 2, GT])
        rest = sb("rest", [128, 2, GT])
        parts = sb("parts", [128, 2, 3, GT], bf16)
        ctxvT = sb("ctxvT", [128, 2 * GP, 2, PAD])
        vals = sb("vals", [128, 2 * GP, HP, VW])

        q6 = sb("q6", [SLOT6, H, GT], bf16)
        k6 = sb("k6", [SLOT6, H, GT], bf16)
        row_max = sb("row_max", [128, GP, H])
        probs = [sb(f"probs{p}", [128, H, PAD]) for p in range(GP)]
        probsT = [sb(f"probsT{p}", [128, HP, 128]) for p in range(GP)]
        rden = sb("rden", [128, GP, H])
        y = sb("y", [128, GP, D])
        yT = sb("yT", [128, GT])

        stat2, mv2 = sb("stat2", [128, GP, 6]), sb("mv2", [128, GP, 2])
        ve2, rs2 = sb("ve2", [128, GP]), sb("rs2", [128, GP])
        rec = sb("rec", [128, TOP_K, GP, REC])
        xn2T = sb("xn2T", [128, GT])
        logit = sb("logit", [128, GP, E])
        lmax = sb("lmax", [128, GP])
        prob = sb("prob", [128, GP, E])
        esum = sb("esum", [128, GP])
        prob2 = sb("prob2", [128, GP, E])
        top = sb("top", [128, TOP_K, GP])
        cand = sb("cand", [128, GP, E])
        pick = sb("pick", [128, GP])
        onehot = sb("onehot", [128, TOP_K, GP, E])
        topsum = sb("topsum", [128, GP])
        taken = sb("taken", [128, GP, E], bf16)
        earlier = sb("earlier", [128, GP, E], bf16)
        over = sb("over", [128, GP, E])
        slot_e = sb("slot_e", [128, GP, E])
        slot_k = sb("slot_k", [128, TOP_K, GP, E])
        slot_i = sb("slot_i", [128, TOP_K, GP], i32)

        w1_s = [sb(f"w1_s{i}", [128, FF]) for i in range(2)]
        w2_s = [sb(f"w2_s{i}", [128, FC, D]) for i in range(2)]
        xg = [sb(f"xg{i}", [SLOT_TILE, SLOT_TILES, REC]) for i in range(2)]
        xgT = [sb(f"xgT{i}", [128, SLOTS]) for i in range(2)]
        hid = [sb(f"hid{i}", [128, FC, SLOTS]) for i in range(2)]
        obias = sb("obias", [SLOT_TILE, SLOT_TILES, D])
        ow = [sb(f"ow{i}", [SLOT_TILE, SLOT_TILES, D]) for i in range(2)]
        far_s = sb("far_s", [SLOT_TILE, SLOT_TILES])
        dst_i = [sb(f"dst_i{i}", [SLOT_TILE, SLOT_TILES], i32) for i in range(2)]

        chosen = sb("chosen", [128, TOP_K, PAIRS, D])
        zeros = chosen[:].rearrange("p k n d -> p (k n d)")[:, 0:N_DST]

        bank = [stack.enter_context(nc.psum_tensor(f"bank{i}", [128, 512], f32)) for i in range(8)]
        score_b = [[bank[0], bank[1]], [bank[2], bank[0]]]
        probT_b = bank[4:6]
        post_b, front_b, mix_b = bank[3], bank[6], bank[7]
        av_p = mix_b[:, 0:HP * VW]
        post_p = post_b[:, 0:GT]
        gate_p = post_b[:, GT:GT + GP * E]
        rank_p = post_b[:, GT + GP * E:GT + 2 * GP * E]

        x_in, w_in, wl_in, mask_in = sem("x_in"), sem("w_in"), sem("wl_in"), sem("mask_in")
        ctxk_in, ctxv_in, stacks_in, parts_out = (sem(n) for n in ("ctxk_in", "ctxv_in", "stacks_in", "parts_out"))
        zero_out, mean_out, slow_dma, slow_step = (sem(n) for n in ("zero_out", "mean_out", "slow_dma", "slow_step"))
        passed = {n: sem(f"passed_{n}") for n in ("dve", "pool")}
        cleared, const_step, const_done, bias_step, bias_done = (
            sem(n) for n in ("cleared", "const_step", "const_done", "bias_step", "bias_done"))
        ident_done, vconst = sem("ident_done"), sem("vconst")
        kept_done, flag_step, flag_done, bqs_done = (sem(n) for n in ("kept_done", "flag_step", "flag_done", "bqs_done"))
        stat1_d, mv1_d, ve1_d, rs1_d, xn_d = (sem(n) for n in ("stat1_d", "mv1_d", "ve1_d", "rs1_d", "xn_d"))
        frontT_d, frontT_ev, qk_d, qk_ev = (sem(n) for n in ("frontT_d", "frontT_ev", "qk_d", "qk_ev"))
        hi_d, rest_d, mid_d, lo_d = (sem(n) for n in ("hi_d", "rest_d", "mid_d", "lo_d"))
        vT_d, vT_ev, v_d, vals_d = (sem(n) for n in ("vT_d", "vT_ev", "v_d", "vals_d"))
        score_d, max_d, sub_d, exp_d = (sem(n) for n in ("score_d", "max_d", "sub_d", "exp_d"))
        probT_d, probT_ev, av_d, rden_d, y_d = (sem(n) for n in ("probT_d", "probT_ev", "av_d", "rden_d", "y_d"))
        yT_d, yT_ev, o_d, xbo_d, x2_d = (sem(n) for n in ("yT_d", "yT_ev", "o_d", "xbo_d", "x2_d"))
        stat2_d, mv2_d, ve2_d, rs2_d, xn2_d = (sem(n) for n in ("stat2_d", "mv2_d", "ve2_d", "rs2_d", "xn2_d"))
        xn2T_d, xn2T_ev, gate_d, lsub_d, lexp_d = (sem(n) for n in ("xn2T_d", "xn2T_ev", "gate_d", "lsub_d", "lexp_d"))
        route, taken_d, rank_d, rec_d, slot_d, disp_out = (
            sem(n) for n in ("route", "taken_d", "rank_d", "rec_d", "slot_d", "disp_out"))
        we_in = [sem(f"we_in{i}") for i in range(2)]
        xg_in = [sem(f"xg_in{i}") for i in range(2)]
        xgT_d, xgT_ev, up_d, hid_a, hid_v = (sem(n) for n in ("xgT_d", "xgT_ev", "up_d", "hid_a", "hid_v"))
        down_d, far_d, dst_d, obias_d, ow_d = (sem(n) for n in ("down_d", "far_d", "dst_d", "obias_d", "ow_d"))
        comb_out = [sem(f"comb_out{i}") for i in range(2)]
        chosen_in = [sem(f"chosen_in{c}") for c in range(PAIRS // 4)]
        sum_step, out_d, out_out = (sem(n) for n in ("sum_step", "out_d", "out_out"))

        block = stack.enter_context(nc.Block())

        def pipeline(eng, it):
            first, last = 1, GROUPS - 3
            for g in range(-3, first):
                it(g, g)
            with eng.Fori(first, last) as g:
                it(g, first)
            for g in range(last, GROUPS + 1):
                it(g, g)

        def stages(s):
            return (s + 3 < GROUPS, 0 <= s + 2 < GROUPS, 0 <= s + 1 < GROUPS, 0 <= s < GROUPS, 0 <= s - 1)

        xv = x.rearrange("(n j) q d -> j q n d", j=2)
        cv = ctx.rearrange("(n j) k d -> j k n d", j=2)
        mean_v = mean_d.rearrange("(n j) (o d) -> j o n d", j=2, o=1)
        maskv = mask.rearrange("(n j) q k -> j q n k", j=2)
        slots_v = slots_d.rearrange("(e t p) r -> e p t r", t=SLOT_TILES, p=SLOT_TILE)
        outv = out.rearrange("(n j) q d -> j q n d", j=2)
        choice_v = choice_d.rearrange("(k n j q) d -> k j q n d", k=TOP_K, j=2, q=S)
        w1v = w1
        w2v = w2.rearrange("e (f p) d -> e p f d", p=128)

        @block.sync
        def _(sp):
            sp.wait_ge(cleared, 1)
            for j in range(2):
                sp.dma_start(m8[PAD * j:PAD * j + S, :, :], maskv[j, :, :, 0:S]).then_inc(mask_in, 16)
            sp.wait_ge(cleared, 2)
            for j in range(2):
                sp.dma_start(xs[PAD * j:PAD * j + S, :, :], xv[j]).then_inc(x_in, 16)
            for to, frm in ((wq_s, wq), (wk_s, wk)):
                sp.dma_start(to[:], frm).then_inc(w_in, 16)
            sp.dma_start(bq_s[:], bq.rearrange("(p o) -> p o", o=1)).then_inc(w_in, 16)
            sp.dma_start(bk_s[:], bk.rearrange("(p o) -> p o", o=1)).then_inc(w_in, 16)
            sp.wait_ge(cleared, 3)
            for j in range(2):
                sp.dma_start(ctxk[PAD * j:PAD * j + S, :, :], cv[j, 0:S, 0:GP, :]).then_inc(ctxk_in, 16)
                sp.dma_start(ctxv[PAD * j:PAD * j + S, :, :], cv[j, 0:S, 0:GP, :]).then_inc(ctxv_in, 16)
            for to, frm in ((wv_s, wv), (wo_s, wo), (gw_s, gate_w)):
                sp.dma_start(to[:], frm).then_inc(wl_in, 16)
            for to, frm in ((bv_s, bv), (bo_s, bo), (gb_s, gate_b)):
                sp.dma_start(to[:], frm.partition_broadcast(128)).then_inc(wl_in, 16)
            sp.dma_start(b1_s[:], b1).then_inc(wl_in, 16)
            sp.dma_start(b2_s[:], b2.rearrange("e d -> (e d)").partition_broadcast(128)
                         .rearrange("p (e d) -> p e d", e=E)).then_inc(wl_in, 16)
            for i in range(2):
                sp.dma_start(w1_s[i][:], w1v[i]).then_inc(we_in[i], 16)
                sp.dma_start(w2_s[i][:], w2v[i]).then_inc(we_in[i], 16)
            sp.wait_ge(mean_out, 16)
            for j in range(2):
                r = PAD * j + S
                sp.dma_start(ctxk[r:r + 1, :, :], mean_v[j, :, 0:GP, :]).then_inc(ctxk_in, 16)
                sp.dma_start(ctxv[r:r + 1, :, :], mean_v[j, :, 0:GP, :]).then_inc(ctxv_in, 16)
            sp.wait_ge(cleared, 4)
            sp.dma_start(slots_d.rearrange("(p a) r -> p (a r)", p=128),
                         zeros[:, 0:E * SLOTS * REC // 128]).then_inc(zero_out, 16)
            sp.dma_start(choice_d.rearrange("(p a) r -> p (a r)", p=128), zeros).then_inc(zero_out, 16)

            def load_context(tile, signal, t):
                for j in range(2):
                    r = PAD * j + S
                    sp.dma_start(tile[PAD * j:r, :, :], cv[j, 0:S, bass.ds(GP * t, GP), :]).then_inc(signal, 16)
                    sp.dma_start(tile[r:r + 1, :, :], mean_v[j, :, bass.ds(GP * t, GP), :]).then_inc(signal, 16)

            def it(g, s):
                norm, front, values, attn, router = stages(s)
                if norm and s > -3:
                    wait(sp, frontT_d, g + 3)
                    load_context(ctxk, ctxk_in, g + 3)
                if values:
                    wait(sp, score_d, 4 * g + 4)
                    sp.wait_ge(parts_out, 16 * (g + 2))
                    for to, which, runs in ((q6, 0, Q_RUNS), (k6, 1, K_RUNS)):
                        for at, part, n in runs:
                            sp.dma_start(to[HD * at:HD * (at + n), :, :],
                                         parts_d[g + 1, which, part:part + n]
                                         .rearrange("s (d h) t -> (s d) h t", h=H)).then_inc(stacks_in, 16)
                if values and s + 2 < GROUPS:
                    sp.wait_ge(vT_d, g + 2)
                    load_context(ctxv, ctxv_in, g + 2)
                if front:
                    sp.wait_ge(lo_d, g + 3)
                    sp.dma_start(parts_d[g + 2].rearrange("w s c t -> c (w s) t"),
                                 parts[:].rearrange("c w s t -> c (w s) t")).then_inc(parts_out, 16)

            pipeline(sp, it)

            def load_expert(e, i, first):
                if not first:
                    sp.wait_ge(down_d, SLOT_TILES * (e - 1))
                    sp.dma_start(w1_s[i][:], w1v[e]).then_inc(we_in[i], 16)
                    sp.dma_start(w2_s[i][:], w2v[e]).then_inc(we_in[i], 16)
                    sp.wait_ge(ow_d, e - 1)
                sp.dma_start(xg[i][:], slots_v[e]).then_inc(xg_in[i], 16)

            sp.wait_ge(disp_out, 16 * TOP_K * PAIRS)
            load_expert(0, 0, True)
            load_expert(1, 1, True)
            with sp.Fori(1, E // 2) as two:
                load_expert(2 * two, 0, False)
                load_expert(2 * two + 1, 1, False)
            for i in range(2):
                sp.wait_ge(comb_out[i], 16 * SLOT_TILES * E // 2)
            for n in range(0, PAIRS, 4):
                for k in range(TOP_K):
                    for j in range(2):
                        sp.dma_start(chosen[PAD * j:PAD * j + S, k, n:n + 4, :],
                                     choice_v[k, j, :, n:n + 4, :]).then_inc(chosen_in[n // 4], 16)
                if n:
                    sp.wait_ge(out_d, n // 4)
                    for j in range(2):
                        sp.dma_start(outv[j, :, n - 4:n, :], x2[PAD * j:PAD * j + S, n - 4:n, :]).then_inc(out_out, 16)
            sp.wait_ge(out_d, PAIRS // 4)
            for j in range(2):
                sp.dma_start(outv[j, :, PAIRS - 4:, :], x2[PAD * j:PAD * j + S, PAIRS - 4:, :]).then_inc(out_out, 16)
            sp.wait_ge(out_out, 32 * PAIRS // 4)
            sp.wait_ge(parts_out, 16 * GROUPS)
            sp.wait_ge(zero_out, 32)

        @block.gpsimd
        def _(pool):
            gp = nc.gpsimd
            gp.memset(causal[:], 1.0).then_inc(const_step, 1)
            gp.memset(ident[:], 0.0).then_inc(const_step, 1)
            gp.memset(before[:], 1.0).then_inc(const_step, 1)
            pool.wait_ge(const_step, 3)
            gp.affine_select(out=ident[:], in_=ident[:], compare_op=ALU.not_equal, fill=1.0, base=0,
                             pattern=[[-1, 128]], channel_multiplier=1).then_inc(ident_done, 1)
            gp.affine_select(out=before[:], in_=before[:], compare_op=ALU.is_ge, fill=0.0, base=0,
                             pattern=[[1, 128]], channel_multiplier=-1).then_inc(const_step, 1)
            gp.memset(minus_half[:], -0.5).then_inc(const_step, 1)
            gp.iota(slot_base_i[:], [[SLOTS, E]], base=-1, channel_multiplier=0).then_inc(const_step, 1)
            gp.iota(order_i[:], [[-1, E]], base=E, channel_multiplier=0).then_inc(const_step, 1)
            gp.iota(dest_i[:], [[B * S, TOP_K], [2 * S, PAIRS]], base=1, channel_multiplier=1).then_inc(const_step, 1)
            gp.memset(mean[:], 0.0).then_inc(const_step, 1)
            for j in range(2):
                pool.wait_ge(const_step, 9 + j)
                gp.affine_select(out=causal[PAD * j:PAD * (j + 1)], in_=causal[PAD * j:PAD * (j + 1)],
                                 compare_op=ALU.is_ge, fill=0.0, base=0, pattern=[[-1, S]],
                                 channel_multiplier=1).then_inc(const_step, 1)
            pool.wait_ge(const_step, 11)

            pool.wait_ge(flag_done, 1)
            flag = pool.value_load(all_gone[0:1, 0:1], min_val=0, max_val=1)
            with pool.If(flag > 0):
                gp.memset(key_sum[:], 0.0).then_inc(slow_step, 1)
                quarters = ctx.rearrange("b (w c k) d -> (b w) c k d", w=KQ, k=KCH)
                with pool.Fori(0, N_KCH) as c:
                    pool.wait_ge(slow_step, c * KCH + 1)
                    pool.dma_start(keys_c[:], quarters[:, c]).then_inc(slow_dma, 16)
                    pool.wait_ge(slow_dma, c * 16 + 16)
                    hold(pool, passed["pool"])
                    with pool.Fori(0, KCH) as k:
                        pool.wait_ge(slow_step, c * KCH + k + 1)
                        gp.tensor_tensor(key_sum[:], key_sum[:], keys_c[:, k, :], add).then_inc(slow_step, 1)
                pool.wait_ge(slow_step, N_KCH * KCH + 1)
                pool.dma_start(sums_d, key_sum[:]).then_inc(slow_dma, 16)
                pool.wait_ge(slow_dma, 16 * N_KCH + 16)
                pool.dma_start(quarter[:], sums_d.rearrange("(b w) d -> b w d", w=KQ)).then_inc(slow_dma, 16)
                pool.wait_ge(slow_dma, 16 * N_KCH + 32)
                for w in range(KQ):
                    gp.tensor_tensor(mean[:], mean[:], quarter[:, w, :], add).then_inc(slow_step, 1)
                    pool.wait_ge(slow_step, N_KCH * KCH + 2 + w)
                gp.tensor_scalar(mean[:], mean[:], 1.0 / S2, None, mult).then_inc(slow_step, 1)
                pool.wait_ge(slow_step, N_KCH * KCH + 2 + KQ)
            pool.dma_start(mean_d, mean[:]).then_inc(mean_out, 16)

            def it(g, s):
                norm, front, values, attn, router = stages(s)
                if front:
                    if s == -2:
                        pool.wait_ge(x_in, 32)
                        pool.wait_ge(wl_in, 128)
                    tiles = bass.ds(GP * (g + 2), GP)
                    for p in range(GP):
                        gp.tensor_tensor(x2[:, GP * (g + 2) + p, :], xs[:, GP * (g + 2) + p, :], bo_s[:], add)\
                            .then_inc(xbo_d, 1)
                    pool.wait_ge(hi_d, g + 3)
                    gp.tensor_tensor(rest[:], qk[:], parts[:, :, 0, :], sub).then_inc(rest_d, 1)
                    pool.wait_ge(mid_d, g + 3)
                    pool.wait_ge(rest_d, g + 3)
                    gp.tensor_tensor(parts[:, :, 2, :], rest[:], parts[:, :, 1, :], sub).then_inc(lo_d, 1)
                if router:
                    pool.wait_ge(ve2_d, g)
                    gp.tensor_tensor(rs2[:], ve2[:], minus_half[:], ALU.pow).then_inc(rs2_d, 1)
                if norm:
                    pool.wait_ge(ve1_d, g + 4)
                    gp.tensor_tensor(rs1[:], ve1[:], minus_half[:], ALU.pow).then_inc(rs1_d, 1)
                if router:
                    pool.wait_ge(xn2_d, GP * g)
                    hold(pool, passed["pool"])
                    gp.tensor_copy(rec[:, 1, :, 0:D], rec[:, 0, :, 0:D]).then_inc(rec_d, 1)
                    gp.tensor_copy(rec[:, :, :, D + 1], dest[:, :, bass.ds(GP * (g - 1), GP)]).then_inc(rec_d, 1)
                    pool.wait_ge(rec_d, 3 * g)
                    pool.wait_ge(slot_d, g)
                    hold(pool, passed["pool"])
                    if s == 1:
                        pool.wait_ge(zero_out, 32)
                    for p in range(GP):
                        for k in range(TOP_K):
                            gp.indirect_dma_start(
                                out=slots_d, out_offset=bass.IndirectOffsetOnAxis(ap=slot_i[:, k, p:p + 1], axis=0),
                                in_=rec[:, k, p, :], in_offset=None, bounds_check=E * SLOTS - 1,
                                oob_is_err=False).then_inc(disp_out, 16)

            pipeline(pool, it)

            def send(e, i, n):
                pool.wait_ge(ow_d, e + 1)
                hold(pool, passed["pool"])
                for t in range(SLOT_TILES):
                    gp.indirect_dma_start(
                        out=choice_d, out_offset=bass.IndirectOffsetOnAxis(ap=dst_i[i][:, t:t + 1], axis=0),
                        in_=ow[i][:, t, :], in_offset=None, bounds_check=N_DST - 1,
                        oob_is_err=False).then_inc(comb_out[i], 16)

            with pool.Fori(0, E // 2) as two:
                send(2 * two, 0, 0)
                send(2 * two + 1, 1, 0)

        @block.scalar
        def _(act):
            sc = nc.scalar

            def it(g, s):
                norm, front, values, attn, router = stages(s)
                if front:
                    act.wait_ge(frontT_d, g + 3)
                    sc.activation(frontT[:].rearrange("p a t -> p (a t)"), front_b[:], ACT.Copy).then_inc(frontT_ev, 1)
                if attn:
                    act.wait_ge(sub_d, 4 * g + 2)
                    sc.activation(probs[0][:, :, 0:KEYS], probs[0][:, :, 0:KEYS], ACT.Exp).then_inc(exp_d, 1)
                if router:
                    act.wait_ge(yT_d, g)
                    sc.activation(yT[:], post_p, ACT.Copy).then_inc(yT_ev, 1)
                if front:
                    if s == -2:
                        act.wait_ge(bqs_done, 1)
                        act.wait_ge(w_in, 64)
                    act.wait_ge(qk_d, g + 3)
                    wait(act, lo_d, g + 2)
                    sc.activation(qk[:, 0, :], front_b[:, 0:GT], ACT.Identity, bias=bqs[:],
                                  scale=float(1.0 / np.sqrt(np.float32(HD)))).then_inc(qk_ev, 1)
                    sc.activation(qk[:, 1, :], front_b[:, GT:2 * GT], ACT.Identity, bias=bk_s[:])\
                        .then_inc(qk_ev, 1)

                def evacuate(p):
                    for i in range(2):
                        act.wait_ge(probT_d, 4 * g + 2 * p + i + 1)
                        sc.activation(probsT[p][:, 4 * i:4 * i + 4, :].rearrange("a h q -> a (h q)"), probT_b[i][:],
                                      ACT.Copy).then_inc(probT_ev, 1)

                if attn:
                    evacuate(0)
                    act.wait_ge(sub_d, 4 * g + 4)
                    sc.activation(probs[1][:, :, 0:KEYS], probs[1][:, :, 0:KEYS], ACT.Exp).then_inc(exp_d, 1)
                if values:
                    act.wait_ge(vT_d, g + 2)
                    for n in range(2):
                        last = sc.activation(ctxvT[:, :, n, :],
                                             front_b[:, 0:GT].rearrange("p (b k) -> p b k", k=PAD), ACT.Copy)
                        last.then_inc(vT_ev, 1)
                if router:
                    act.wait_ge(xn2T_d, g)
                    sc.activation(xn2T[:], post_p, ACT.Copy).then_inc(xn2T_ev, 1)
                if attn:
                    evacuate(1)
                if router:
                    act.wait_ge(lsub_d, g)
                    sc.activation(prob[:], logit[:], ACT.Exp).then_inc(lexp_d, 1)

            pipeline(act, it)

            def expert(e, i):
                act.wait_ge(xgT_d, e + 1)
                sc.activation(xgT[i][:], probT_b[i][:, 0:SLOTS], ACT.Copy).then_inc(xgT_ev, 1)
                for f in (0, 2):
                    act.wait_ge(up_d, FC * e + f + 1)
                    sc.activation(hid[i][:, f, :], bank[f][:, 0:SLOTS], ACT.Relu, bias=b1_s[:, e, f:f + 1])\
                        .then_inc(hid_a, 1)

            with act.Fori(0, E // 2) as two:
                expert(2 * two, 0)
                expert(2 * two + 1, 1)

        @block.vector
        def _(dve):
            ve = nc.vector

            def constants():
                dve.wait_ge(ident_done, 1)
                ve.tensor_copy(ident_b[:], ident[:]).then_inc(vconst, 1)
                ve.reduce_sum(row_ok[:], ident[:].rearrange("p (j q) -> p j q", j=2)[:, :, 0:S], mybir.AxisListType.XY)\
                    .then_inc(vconst, 1)
                ve.memset(valid[:], 1.0).then_inc(vconst, 1)
                dve.wait_ge(const_step, 9)
                dve.wait_ge(vconst, 3)
                ve.tensor_scalar(before[:], before[:], row_ok[:], None, mult).then_inc(vconst, 1)
                ve.tensor_scalar(valid[:], valid[:], row_ok[:], None, mult).then_inc(vconst, 1)
                ve.tensor_scalar(row_far[:], row_ok[:], -FAR, FAR, mult, add).then_inc(vconst, 1)
                ve.tensor_copy(order[:], order_i[:]).then_inc(vconst, 1)
                ve.tensor_copy(dest[0:PAD], dest_i[0:PAD]).then_inc(vconst, 1)
                ve.tensor_scalar(dest[PAD:128], dest_i[PAD:128], float(S - PAD), None, add).then_inc(vconst, 1)
                dve.wait_ge(vconst, 9)
                ve.tensor_scalar(slot_base[:], slot_base_i[:], row_far[:], None, add).then_inc(const_done, 1)

            ve.memset(m8[:].rearrange("p a b -> p (a b)").bitcast(i32), 0).then_inc(cleared, 1)
            ve.memset(xs[:], 0.0).then_inc(cleared, 1)
            ve.memset(ctxk[:], 0.0)
            ve.memset(ctxv[:], 0.0).then_inc(cleared, 1)
            def mask_to_bias():
                dve.wait_ge(mask_in, 32)
                dve.wait_ge(const_step, 11)
                ve.tensor_tensor(mc[:], m8[:], causal[:].unsqueeze(1).broadcast_to([128, PAIRS, S]), mult)\
                    .then_inc(bias_step, 1)
                ve.memset(bias[:], GONE).then_inc(bias_step, 1)
                dve.wait_ge(bias_step, 2)
                ve.reduce_max(some[:], mc[:], X).then_inc(bias_step, 1)
                dve.wait_ge(bias_step, 3)
                ve.tensor_scalar(bias[:, :, 0:S], mc[:], -1.0, -GONE, add, mult)
                ve.tensor_scalar(bias[:, :, S], some[:], GONE, None, mult).then_inc(bias_done, 1)
                dve.wait_ge(kept_done, 1)
                ve.reduce_sum(rows_kept[:], mix_b[0:1, 0:PAIRS], X).then_inc(flag_step, 1)
                dve.wait_ge(flag_step, 1)
                ve.tensor_scalar(all_gone[:], rows_kept[:], B * S - 0.5, None, ALU.is_lt).then_inc(flag_done, 1)
            constants()
            mask_to_bias()
            dve.wait_ge(x_in, 32)

            def norm_stats(t, tiles, stat, mv, vee, stat_d, mv_d, ve_d):
                for p in range(GP):
                    ve.bn_stats(stat[:, p, :], tiles[:, GP * t + p, :]).then_inc(stat_d, 1)
                wait(dve, stat_d, GP * (t + 1))
                hold(dve, passed["dve"])
                for p in range(GP):
                    ve.bn_aggr(mv[:, p, :], stat[:, p, :]).then_inc(mv_d, 1)
                wait(dve, mv_d, GP * (t + 1))
                ve.tensor_scalar(vee[:], mv[:, :, 1], 1e-5, None, add).then_inc(ve_d, 1)

            def clear_buffers():
                dve.wait_ge(w_in, 64)
                ve.tensor_scalar(bqs[:], bq_s[:], float(1.0 / np.sqrt(np.float32(HD))), None, mult)\
                    .then_inc(bqs_done, 1)
                ve.memset(chosen[:], 0.0).then_inc(cleared, 1)
                for p in range(GP):
                    ve.memset(probs[p][:], 0.0)
                ve.memset(earlier[:], 0.0).then_inc(cleared, 1)
                ve.memset(vals[:], 0.0).then_inc(cleared, 1)
                dve.wait_ge(cleared, 6)
                ve.memset(vals[0:PAD, :, :, HD], 1.0)
                ve.memset(vals[PAD:128, :, :, VW - 1], 1.0).then_inc(cleared, 1)
                dve.wait_ge(wl_in, 128)

            def it(g, s):
                norm, front, values, attn, router = stages(s)

                def softmax_in(p):
                    wait(dve, probT_d, 4 * (g - 1) + 2 * p + 2)
                    for i in range(2):
                        unit = 4 * g + 2 * p + i
                        scores = score_b[p][i][:].rearrange("q (h k) -> q h k", k=PAD)[:, :, 0:KEYS]
                        maxima = row_max[:, p, 8 * i:8 * i + 8]
                        dve.wait_ge(score_d, unit + 1)
                        ve.reduce_max(maxima, scores, X).then_inc(max_d, 1)
                        dve.wait_ge(max_d, unit + 1)
                        ve.tensor_tensor(probs[p][:, 8 * i:8 * i + 8, 0:KEYS], scores,
                                         maxima.unsqueeze(2).broadcast_to([128, 8, KEYS]), sub).then_inc(sub_d, 1)

                def divide(p, t):
                    dve.wait_ge(av_d, 2 * t + p + 1)
                    heads = av_p.rearrange("q (h d) -> q h d", d=HD + 1)
                    ve.reciprocal(rden[:, p, :], heads[:, :, HD]).then_inc(rden_d, 1)
                    dve.wait_ge(rden_d, 2 * t + p + 1)
                    ve.tensor_tensor(y[:, p, :].rearrange("q (h d) -> q h d", d=HD), heads[:, :, 0:HD],
                                     rden[:, p, :].unsqueeze(2).broadcast_to([128, H, HD]), mult).then_inc(y_d, 1)

                if router:
                    divide(1, g - 1)
                if s == -2:
                    clear_buffers()
                if attn:
                    softmax_in(0)
                    dve.wait_ge(v_d, g + 1)
                    wait(dve, av_d, 2 * g)
                    for j in range(2):
                        half = slice(PAD * j, PAD * (j + 1))
                        last = ve.tensor_tensor(
                            vals[half, :, :, (HD + 1) * j:(HD + 1) * j + HD],
                            front_b[half, :].rearrange("k (b h two d) -> k b h two d", b=2 * GP, two=2, d=HD)[:, :, :, j, :],
                            bv_s[half, :].rearrange("k (h two d) -> k h two d", two=2, d=HD)[:, :, j, :]
                            .unsqueeze(1).broadcast_to([PAD, 2 * GP, HP, HD]), add)
                        last.then_inc(vals_d, 1)
                if front:
                    dve.wait_ge(qk_ev, 2 * (g + 3))
                    wait(dve, parts_out, 16 * (g + 2))
                    ve.tensor_copy(parts[:, :, 0, :], qk[:]).then_inc(hi_d, 1)
                if attn:
                    softmax_in(1)
                if front:
                    dve.wait_ge(rest_d, g + 3)
                    ve.tensor_copy(parts[:, :, 1, :], rest[:]).then_inc(mid_d, 1)
                if router:
                    t = g - 1
                    dve.wait_ge(o_d, g)
                    dve.wait_ge(xbo_d, GP * g)
                    tiles = x2[:, bass.ds(GP * t, GP), :].rearrange("q p d -> q (p d)")
                    ve.tensor_tensor(tiles, tiles, post_p, add).then_inc(x2_d, 1)
                    dve.wait_ge(x2_d, g)
                    hold(dve, passed["dve"])
                    norm_stats(t, x2, stat2, mv2, ve2, stat2_d, mv2_d, ve2_d)
                if norm:
                    norm_stats(g + 3, xs, stat1, mv1, ve1, stat1_d, mv1_d, ve1_d)
                if router:
                    dve.wait_ge(rs2_d, g)
                    wait(dve, disp_out, 64 * (g - 1))
                    for p in range(GP):
                        ve.tensor_scalar(rec[:, 0, p, 0:D], x2[:, GP * t + p, :], mv2[:, p, 0:1], rs2[:, p:p + 1],
                                         sub, mult).then_inc(xn2_d, 1)
                if attn:
                    divide(0, g)
                if norm:
                    dve.wait_ge(rs1_d, g + 4)
                    wait(dve, frontT_d, g + 3)
                    for p in range(GP):
                        last = ve.tensor_scalar(xn[:, p, :], xs[:, GP * (g + 3) + p, :], mv1[:, p, 0:1],
                                                rs1[:, p:p + 1], sub, mult)
                    last.then_inc(xn_d, 1)
                if router:
                    steps = [0]

                    def step(ins):
                        steps[0] += 1
                        ins.then_inc(route, 1)

                    def after():
                        dve.wait_ge(route, ROUTE * (g - 1) + steps[0])

                    def per_tile(ap):
                        return ap.unsqueeze(2).broadcast_to([128, GP, E])

                    order_v = order[:].unsqueeze(1).broadcast_to([128, GP, E])
                    dve.wait_ge(gate_d, g)
                    step(ve.tensor_tensor(logit[:], gate_p.rearrange("q (p e) -> q p e", e=E),
                                          gb_s[:].unsqueeze(1).broadcast_to([128, GP, E]), add))
                    after()
                    step(ve.reduce_max(lmax[:], logit[:], X))
                    after()
                    ve.tensor_tensor(logit[:], logit[:], per_tile(lmax[:]), sub).then_inc(lsub_d, 1)
                    dve.wait_ge(lexp_d, g)
                    step(ve.reduce_sum(esum[:], prob[:], X))
                    after()
                    step(ve.reciprocal(esum[:], esum[:]))
                    after()
                    step(ve.tensor_tensor(prob[:], prob[:], per_tile(esum[:]), mult))
                    after()
                    src = prob
                    for k in range(TOP_K):
                        step(ve.reduce_max(top[:, k, :], src[:], X))
                        after()
                        step(ve.tensor_tensor(cand[:], src[:], per_tile(top[:, k, :]), ALU.is_equal))
                        after()
                        step(ve.tensor_tensor(cand[:], cand[:], order_v, mult))
                        after()
                        step(ve.reduce_max(pick[:], cand[:], X))
                        after()
                        step(ve.tensor_tensor(onehot[:, k], order_v, per_tile(pick[:]), ALU.is_equal))
                        after()
                        if k == 0:
                            step(ve.scalar_tensor_tensor(prob2[:], onehot[:, 0], -4.0, prob[:], mult, add))
                            after()
                            src = prob2
                    ve.tensor_tensor(taken[:], onehot[:, 0], onehot[:, 1], add).then_inc(taken_d, 1)
                    step(ve.tensor_tensor(topsum[:], top[:, 0, :], top[:, 1, :], add))
                    dve.wait_ge(taken_d, 2 * g - 1)
                    ve.tensor_tensor(earlier[:, 1, :], earlier[:, 0, :], taken[:, 0, :], add).then_inc(taken_d, 1)
                    after()
                    step(ve.reciprocal(topsum[:], topsum[:]))
                    after()
                    ve.tensor_tensor(rec[:, :, :, D], top[:], topsum[:].unsqueeze(1).broadcast_to([128, TOP_K, GP]),
                                     mult).then_inc(rec_d, 1)
                    dve.wait_ge(rank_d, g)
                    rank = rank_p.rearrange("q (p e) -> q p e", e=E)
                    step(ve.tensor_scalar(over[:], rank, CAP + 0.5, FAR, ALU.is_gt, mult))
                    step(ve.tensor_tensor(earlier[:, 0, :], earlier[:, 1, :], taken[:, 1, :], add))
                    step(ve.tensor_tensor(slot_e[:], rank, slot_base[:].unsqueeze(1).broadcast_to([128, GP, E]), add))
                    after()
                    step(ve.tensor_tensor(slot_e[:], slot_e[:], over[:], add))
                    after()
                    step(ve.tensor_tensor(slot_k[:], onehot[:], slot_e[:].unsqueeze(1)
                                          .broadcast_to([128, TOP_K, GP, E]), mult))
                    after()
                    with nc.allow_low_precision(reason="slots are whole numbers, summed in float32"):
                        ve.reduce_sum(slot_i[:], slot_k[:], X).then_inc(slot_d, 1)
                    assert steps[0] == ROUTE, steps

            ROUTE = 23
            pipeline(dve, it)

            def expert(e, i):
                dve.wait_ge(xg_in[i], 8 * (e - i) + 16)
                wait(dve, comb_out[i], 8 * SLOT_TILES * (e - i))
                ve.tensor_scalar(far_s[:], xg[i][:, :, D + 1], 0.5, FAR, ALU.is_lt, mult).then_inc(far_d, 1)
                dve.wait_ge(far_d, e + 1)
                ve.scalar_tensor_tensor(dst_i[i][:], xg[i][:, :, D + 1], -1.0, far_s[:], add, add).then_inc(dst_d, 1)
                for f in (1, 3):
                    dve.wait_ge(up_d, FC * e + f + 1)
                    ve.tensor_scalar(hid[i][:, f, :], bank[f][:, 0:SLOTS], b1_s[:, e, f:f + 1], 0.0, add, ALU.max)\
                        .then_inc(hid_v, 1)
                dve.wait_ge(down_d, SLOT_TILES * (e + 1))
                ve.tensor_tensor(obias[:], bank[6 + i][0:SLOT_TILE, 0:SLOT_TILES * D].rearrange("s (t d) -> s t d", d=D),
                                 b2_s[0:SLOT_TILE, e, :].unsqueeze(1).broadcast_to([SLOT_TILE, SLOT_TILES, D]), add)\
                    .then_inc(obias_d, 1)
                dve.wait_ge(obias_d, e + 1)
                ve.tensor_tensor(ow[i][:], obias[:],
                                 xg[i][:, :, D:D + 1].broadcast_to([SLOT_TILE, SLOT_TILES, D]), mult).then_inc(ow_d, 1)

            with dve.Fori(0, E // 2) as two:
                expert(2 * two, 0)
                expert(2 * two + 1, 1)
            dve.wait_ge(dst_d, E)
            for c in range(PAIRS // 4):
                n = 4 * c
                dve.wait_ge(chosen_in[c], 64)
                ve.tensor_tensor(chosen[:, 0, n:n + 4, :], chosen[:, 0, n:n + 4, :], chosen[:, 1, n:n + 4, :], add)\
                    .then_inc(sum_step, 1)
                dve.wait_ge(sum_step, c + 1)
                ve.tensor_tensor(x2[:, n:n + 4, :], x2[:, n:n + 4, :], chosen[:, 0, n:n + 4, :], add).then_inc(out_d, 1)

        @block.tensor
        def _(pe):
            mm, tr = nc.tensor.matmul, nc.tensor.transpose
            pe.wait_ge(const_done, 1)
            pe.wait_ge(bias_step, 3)
            mm(mix_b[0:1, 0:PAIRS], valid[:, 0:1], some[:], start=True, stop=True).then_inc(kept_done, 1)

            def it(g, s):
                norm, front, values, attn, router = stages(s)

                def scores(p):
                    for i in range(2):
                        wait(pe, sub_d, 4 * g + ((0, -2), (-1, 1))[p][i])
                        rows = bias[:, GP * g + p, :].unsqueeze(1).broadcast_to([128, 8, PAD])
                        mm(score_b[p][i][:], ident_b[:], rows, start=True, stop=False, skip_group_check=True)
                        for h in range(8):
                            for j in range(2):
                                cols = slice(128 * p + PAD * j, 128 * p + PAD * (j + 1))
                                last = mm(score_b[p][i][PAD * j:PAD * (j + 1), PAD * h:PAD * (h + 1)],
                                          q6[:, 8 * i + h, cols], k6[:, 8 * i + h, cols], start=False, stop=True,
                                          skip_group_check=True)
                        last.then_inc(score_d, 1)

                def transpose_probs(p):
                    pe.wait_ge(exp_d, 2 * g + p + 1)
                    for i in range(2):
                        wait(pe, probT_ev, 4 * g + 2 * p + i - 1)
                        for h in range(4):
                            hp = 4 * i + h
                            last = tr(probT_b[i][:, 128 * h:128 * (h + 1)],
                                      probs[p][:, 2 * hp:2 * hp + 2, :].rearrange("q h k -> q (h k)"), ident[:])
                        last.then_inc(probT_d, 1)

                def mix_values(p):
                    pe.wait_ge(probT_ev, 4 * g + 2 * p + 2)
                    pe.wait_ge(vals_d, 2 * (g + 1))
                    wait(pe, y_d, 2 * g + p)
                    for j in range(2):
                        for hp in range(HP):
                            last = mm(av_p[PAD * j:PAD * (j + 1), VW * hp:VW * (hp + 1)],
                                      probsT[p][:, hp, PAD * j:PAD * (j + 1)], vals[:, GP * p + j, hp, :],
                                      start=True, stop=True, skip_group_check=True)
                    last.then_inc(av_d, 1)

                if s == -2:
                    pe.wait_ge(w_in, 64)
                if attn:
                    if s == 0:
                        pe.wait_ge(bias_done, 1)
                        pe.wait_ge(cleared, 7)
                    pe.wait_ge(stacks_in, 16 * N_STACK * (g + 1))
                    scores(0)
                if front:
                    pe.wait_ge(xn_d, g + 3)
                    pe.wait_ge(ctxk_in, 64 * (g + 3))
                    wait(pe, vals_d, 2 * (g + 1))
                    for p in range(GP):
                        tr(front_b[:, 128 * p:128 * (p + 1)], xn[:, p, :], ident[:])
                        last = tr(front_b[:, GT + 128 * p:GT + 128 * (p + 1)], ctxk[:, p, :], ident[:])
                    last.then_inc(frontT_d, 1)
                if attn:
                    scores(1)
                if router:
                    pe.wait_ge(y_d, 2 * g)
                    for p in range(GP):
                        last = tr(post_p[:, 128 * p:128 * (p + 1)], y[:, p, :], ident[:])
                    last.then_inc(yT_d, 1)
                if front:
                    pe.wait_ge(frontT_ev, g + 3)
                    mm(front_b[:, 0:GT], wq_s[:], frontT[:, 0, :], start=True, stop=True)
                    mm(front_b[:, GT:2 * GT], wk_s[:], frontT[:, 1, :], start=True, stop=True).then_inc(qk_d, 1)
                if router:
                    pe.wait_ge(yT_ev, g)
                    for p in range(GP):
                        last = mm(post_p[:, 128 * p:128 * (p + 1)], yT[:, 128 * p:128 * (p + 1)], wo_s[:],
                                  start=True, stop=True)
                    last.then_inc(o_d, 1)
                if attn:
                    transpose_probs(0)
                if values:
                    if s == -1:
                        pe.wait_ge(wl_in, 128)
                    if front:
                        pe.wait_ge(qk_ev, 2 * (g + 3))
                    else:
                        wait(pe, vals_d, 2 * (g + 1))
                    pe.wait_ge(ctxv_in, 64 * (g + 2))
                    for p in range(GP):
                        last = tr(front_b[:, 128 * p:128 * (p + 1)], ctxv[:, p, :], ident[:])
                    last.then_inc(vT_d, 1)
                if attn:
                    mix_values(0)
                if router:
                    pe.wait_ge(xn2_d, GP * g)
                    for p in range(GP):
                        last = tr(post_p[:, 128 * p:128 * (p + 1)], rec[:, 0, p, 0:D], ident[:])
                    last.then_inc(xn2T_d, 1)
                if attn:
                    transpose_probs(1)
                if values:
                    pe.wait_ge(vT_ev, 2 * (g + 2))
                    for b in range(2 * GP):
                        last = mm(front_b[:, D * b:D * (b + 1)], ctxvT[:, b, :, :].rearrange("c n k -> c (n k)"),
                                  wv_s[:], start=True, stop=True)
                    last.then_inc(v_d, 1)
                if router:
                    pe.wait_ge(xn2T_ev, g)
                    for p in range(GP):
                        last = mm(gate_p[:, E * p:E * (p + 1)], xn2T[:, 128 * p:128 * (p + 1)], gw_s[:],
                                  start=True, stop=True)
                    last.then_inc(gate_d, 1)
                if attn:
                    mix_values(1)
                if router:
                    pe.wait_ge(taken_d, 2 * g)
                    mm(rank_p, before[:], taken[:].rearrange("q p e -> q (p e)"), start=True, stop=False)
                    mm(rank_p, valid[:], earlier[:].rearrange("q p e -> q (p e)"), start=False, stop=True)\
                        .then_inc(rank_d, 1)

            pipeline(pe, it)

            def transpose_slots(e, i):
                pe.wait_ge(xg_in[i], 8 * (e - i) + 16)
                wait(pe, xgT_ev, e - 1)
                for t in range(SLOT_TILES):
                    last = tr(probT_b[i][:, SLOT_TILE * t:SLOT_TILE * (t + 1)], xg[i][:, t, 0:D],
                              ident[0:SLOT_TILE, 0:SLOT_TILE])
                last.then_inc(xgT_d, 1)

            def expert(e, i, more):
                pe.wait_ge(we_in[i], 16 * (e - i) + 32)
                pe.wait_ge(xgT_ev, e + 1)
                wait(pe, hid_a, 2 * e)
                wait(pe, hid_v, 2 * e)
                for f in range(FC):
                    mm(bank[f][:, 0:SLOTS], w1_s[i][:, 128 * f:128 * (f + 1)], xgT[i][:], start=True, stop=True)\
                        .then_inc(up_d, 1)
                if more:
                    transpose_slots(e + 1, 1 - i)
                wait(pe, obias_d, e - 1)
                pe.wait_ge(hid_a, 2 * e + 2)
                pe.wait_ge(hid_v, 2 * e + 2)
                for t in range(SLOT_TILES):
                    for f in range(FC):
                        last = mm(bank[6 + i][0:SLOT_TILE, D * t:D * (t + 1)],
                                  hid[i][:, f, SLOT_TILE * t:SLOT_TILE * (t + 1)], w2_s[i][:, f, :],
                                  start=(f == 0), stop=(f == FC - 1))
                    last.then_inc(down_d, 1)

            transpose_slots(0, 0)
            expert(0, 0, True)
            expert(1, 1, True)
            with pe.Fori(1, E // 2 - 1) as two:
                expert(2 * two, 0, True)
                expert(2 * two + 1, 1, True)
            expert(E - 2, 0, True)
            expert(E - 1, 1, False)


def kernel(x, ctx_1024, mask_BxSxS2_bf1, L0_xattn_Wk, L0_xattn_bk, L0_xattn_Wq, L0_xattn_bq, L0_xattn_Wv,
           L0_xattn_bv, L0_xattn_Wo, L0_xattn_bo, L0_ffn_gate_w, L0_ffn_gate_b, L0_ffn_w1, L0_ffn_b1,
           L0_ffn_w2, L0_ffn_b2):
    import concourse.bacc as bacc
    from concourse.bass_utils import run_bass_kernel_spmd

    def by_feature(a):
        a = np.asarray(a)
        return np.ascontiguousarray(a.reshape(*a.shape[:-1], H, HD).swapaxes(-1, -2).reshape(a.shape))

    arrays = {
        "x": np.asarray(x), "ctx": np.asarray(ctx_1024), "mask": np.asarray(mask_BxSxS2_bf1).view(np.uint8),
        "wk": by_feature(L0_xattn_Wk), "bk": by_feature(L0_xattn_bk),
        "wq": by_feature(L0_xattn_Wq), "bq": by_feature(L0_xattn_bq),
        "wv": np.asarray(L0_xattn_Wv), "bv": np.asarray(L0_xattn_bv),
        "wo": np.asarray(L0_xattn_Wo), "bo": np.asarray(L0_xattn_bo),
        "gate_w": np.asarray(L0_ffn_gate_w), "gate_b": np.asarray(L0_ffn_gate_b),
        "w1": np.asarray(L0_ffn_w1),
        "b1": np.ascontiguousarray(np.asarray(L0_ffn_b1).reshape(E, FC, 128).transpose(2, 0, 1)),
        "w2": np.asarray(L0_ffn_w2), "b2": np.asarray(L0_ffn_b2),
    }
    nc = bacc.Bacc("TRN2", target_bir_lowering=False, num_devices=1)
    ins, feed = [], {}
    for name, a in arrays.items():
        a = np.ascontiguousarray(a)
        feed[f"{name}_in"] = a
        ins.append(nc.dram_tensor(f"{name}_in", a.shape, mybir.dt.from_np(a.dtype), kind="ExternalInput").ap())
    out = nc.dram_tensor("out", (B, S, D), mybir.dt.float32, kind="ExternalOutput").ap()
    build(nc, *ins, out)
    return run_bass_kernel_spmd(nc, [feed], core_ids=[0]).results[0]["out"]
```

```python
from contextlib import ExitStack

import numpy as np

import concourse.bass as bass
from concourse import mybir

B, S, S2, D = 32, 56, 1500, 128
H, HD = 16, 8
E, FF, TOP_K = 8, 512, 2
CAP = int(1.25 * B * S / E)
SLOT_TILES = 3
SLOT_TILE = -(-CAP // SLOT_TILES)
SLOTS = SLOT_TILE * SLOT_TILES
PAD = 64
PAIRS = B // 2
GP = 2
GROUPS = PAIRS // GP
GT = GP * 2 * PAD
KEYS = S + 1
HP = H // 2
VW = 2 * (HD + 1)
FC = FF // 128
REC = D + 2
N_DST = PAIRS * TOP_K * 128
FAR = 8192.0
GONE = -1.0e30
PRODUCTS = 6
STACK_WRITES = 7
CHUNK = 4
CHUNKS = range(0, PAIRS, CHUNK)
KQ = 4
KCH = 25
N_KCH = S2 // KQ // KCH


def wait(eng, sem, value):
    if isinstance(value, int) and value <= 0:
        return
    eng.wait_ge(sem, value)


def hold(eng, passed):
    eng.sem_inc(passed, 1)


def build(nc, x, ctx, mask, wk, bk, wq, bq, wv, bv, wo, bo, gate_w, gate_b, w1, b1, w2, b2, out):
    f32, bf16, i32, u8 = mybir.dt.float32, mybir.dt.bfloat16, mybir.dt.int32, mybir.dt.uint8
    ALU, ACT, X = mybir.AluOpType, mybir.ActivationFunctionType, mybir.AxisListType.X
    add, sub, mult = ALU.add, ALU.subtract, ALU.mult

    with ExitStack() as stack:
        def sb(name, shape, dt=f32):
            return stack.enter_context(nc.sbuf_tensor(name, shape, dt))

        def sem(name):
            return stack.enter_context(nc.semaphore(name))

        def dram(name, shape, dt=f32):
            return nc.dram_tensor(name, shape, dt, kind="Internal").ap()

        stacks_d = dram("stacks_d", (GROUPS, 2, PRODUCTS, D, GT), bf16)
        slots_d = dram("slots_d", (E * SLOTS, REC))
        choice_d = dram("choice_d", (N_DST, D))
        sums_d = dram("sums_d", (KQ * B, D))
        ctx_d = dram("ctx_d", (PAIRS, 2, PAD, D))

        ident = sb("ident", [128, 128])
        ident_b = sb("ident_b", [128, 128], bf16)
        causal = sb("causal", [128, S], bf16)
        before = sb("before", [128, 128], bf16)
        valid = sb("valid", [128, 128], bf16)
        slot_base_i = sb("slot_base_i", [128, E], i32)
        slot_base = sb("slot_base", [128, E])
        expert_i = sb("expert_i", [128, E], i32)
        expert_no = sb("expert_no", [128, E])
        dest_i = sb("dest_i", [128, TOP_K, PAIRS], i32)
        dest = sb("dest", [128, TOP_K, PAIRS])
        row_ok, row_far = sb("row_ok", [128, 1]), sb("row_far", [128, 1])
        minus_half = sb("minus_half", [128, GP])
        wq_s, wk_s, wv_s, wo_s = (sb(n, [128, D]) for n in ("wq_s", "wk_s", "wv_s", "wo_s"))
        bq_s, bk_s, bqs = (sb(n, [128, 1]) for n in ("bq_s", "bk_s", "bqs"))
        bv_s, bo_s = sb("bv_s", [128, D]), sb("bo_s", [128, D])
        gw_s, gb_s = sb("gw_s", [128, E]), sb("gb_s", [128, E])
        b1_s = sb("b1_s", [128, E, FC])
        b2_s = sb("b2_s", [128, E, D])
        xs = sb("xs", [128, PAIRS, D])
        x2 = sb("x2", [128, PAIRS, D])
        m8 = sb("m8", [128, PAIRS, S], u8)
        mc = sb("mc", [128, PAIRS, S], bf16)
        some = sb("some", [128, PAIRS], bf16)
        bias = sb("bias", [128, PAIRS, PAD], bf16)
        rows_kept = sb("rows_kept", [1, 1])
        all_gone = sb("all_gone", [1, 1], i32)

        key_sum = sb("key_sum", [128, D])
        keys_c = sb("keys_c", [128, KCH, D])
        quarter = sb("quarter", [B, KQ, D])
        mean = sb("mean", [B, D])

        pad_keys = sb("pad_keys", [B, (PAD - KEYS) * D])
        ctxk = sb("ctxk", [128, GP, D])
        ctxv = sb("ctxv", [128, GP, D])
        stat1, mv1 = sb("stat1", [128, GP, 6]), sb("mv1", [128, GP, 2])
        ve1, rs1, nb1 = (sb(n, [128, GP]) for n in ("ve1", "rs1", "nb1"))
        xn = sb("xn", [128, GP, D])
        frontT = sb("frontT", [128, 2, GT])
        qk = sb("qk", [128, 2, GT])
        rest = sb("rest", [128, 2, GT])
        parts = sb("parts", [128, 2, 3, GT], bf16)
        ctxvT = sb("ctxvT", [128, 2 * GP, 2, PAD])
        vals = sb("vals", [128, 2 * GP, HP, VW])

        q6 = sb("q6", [PRODUCTS * HD, H, GT], bf16)
        k6 = sb("k6", [PRODUCTS * HD, H, GT], bf16)
        row_max = sb("row_max", [128, GP, H])
        probs = [sb(f"probs{p}", [128, H, PAD]) for p in range(GP)]
        probsT = [sb(f"probsT{p}", [128, HP, 128]) for p in range(GP)]
        rden = sb("rden", [128, GP, H])
        y = sb("y", [128, GP, D])
        yT = sb("yT", [128, GT])

        stat2, mv2 = sb("stat2", [128, GP, 6]), sb("mv2", [128, GP, 2])
        ve2, rs2, nb2 = (sb(n, [128, GP]) for n in ("ve2", "rs2", "nb2"))
        xn2 = sb("xn2", [128, GP, D])
        rec = sb("rec", [128, TOP_K, GP, REC])
        xn2T = sb("xn2T", [128, GT])
        logit = sb("logit", [128, GP, E])
        lmax = sb("lmax", [128, GP])
        prob = sb("prob", [128, GP, E])
        esum = sb("esum", [128, GP])
        top = sb("top", [128, GP, E])
        top_i = sb("top_i", [128, GP, E], mybir.dt.uint32)
        weight = sb("weight", [128, TOP_K, GP])
        onehot = sb("onehot", [128, TOP_K, GP, E])
        topsum = sb("topsum", [128, GP])
        taken = sb("taken", [128, GP, E], bf16)
        earlier = sb("earlier", [128, GP, E], bf16)
        over = sb("over", [128, GP, E])
        slot_e = sb("slot_e", [128, GP, E])
        slot_k = sb("slot_k", [128, TOP_K, GP, E])
        slot_i = sb("slot_i", [128, TOP_K, GP], i32)

        w1_s = [sb(f"w1_s{i}", [128, FF]) for i in range(2)]
        w2_s = [sb(f"w2_s{i}", [128, FC, D]) for i in range(2)]
        xg = [sb(f"xg{i}", [SLOT_TILE, SLOT_TILES, REC]) for i in range(2)]
        xgT = [sb(f"xgT{i}", [128, SLOTS]) for i in range(2)]
        hid = [sb(f"hid{i}", [128, FC, SLOTS]) for i in range(2)]
        weight_s = [sb(f"weight_s{i}", [SLOT_TILE, SLOT_TILES]) for i in range(2)]
        obias = sb("obias", [SLOT_TILE, SLOT_TILES, D])
        ow = [sb(f"ow{i}", [SLOT_TILE, SLOT_TILES, D]) for i in range(2)]
        far_s = [sb(f"far_s{i}", [SLOT_TILE, SLOT_TILES]) for i in range(2)]
        dst_i = [sb(f"dst_i{i}", [SLOT_TILE, SLOT_TILES], i32) for i in range(2)]

        chosen = sb("chosen", [128, PAIRS, TOP_K, D])
        zeros = chosen[:].rearrange("p n k d -> p (n k d)")

        bank = [stack.enter_context(nc.psum_tensor(f"bank{i}", [128, 512], f32)) for i in range(8)]
        score_b = [[bank[0], bank[1]], [bank[2], bank[0]]]
        probT_b = bank[4:6]
        post_b, front_b, mix_b = bank[3], bank[6], bank[7]
        av_p = mix_b[:, 0:HP * VW]
        post_p = post_b[:, 0:GT]
        gate_p = post_b[:, GT:GT + GP * E]
        rank_p = mix_b[:, HP * VW:HP * VW + GP * E]

        x_in, w_in, bo_in, wl_in, wb_in, mask_in = (
            sem(n) for n in ("x_in", "w_in", "bo_in", "wl_in", "wb_in", "mask_in"))
        ctxk_in, ctxv_in, stacks_in, parts_out = (sem(n) for n in ("ctxk_in", "ctxv_in", "stacks_in", "parts_out"))
        copy_out, zero_out, mean_out, slow_dma, slow_step = (sem(n) for n in ("copy_out", "zero_out", "mean_out", "slow_dma", "slow_step"))
        passed = {n: sem(f"passed_{n}") for n in ("dve", "pool")}
        cleared, const_step, const_done, bias_step, bias_done = (
            sem(n) for n in ("cleared", "const_step", "const_done", "bias_step", "bias_done"))
        all_clear = sem("all_clear")
        ident_done, vconst = sem("ident_done"), sem("vconst")
        kept_done, flag_step, flag_done, bqs_done = (sem(n) for n in ("kept_done", "flag_step", "flag_done", "bqs_done"))
        stat1_d, mv1_d, ve1_d, rs1_d, nb1_d, xn_d = (
            sem(n) for n in ("stat1_d", "mv1_d", "ve1_d", "rs1_d", "nb1_d", "xn_d"))
        frontT_d, frontT_ev, qk_d, qk_ev = (sem(n) for n in ("frontT_d", "frontT_ev", "qk_d", "qk_ev"))
        hi_d, rest_d, mid_d, lo_d = (sem(n) for n in ("hi_d", "rest_d", "mid_d", "lo_d"))
        vT_d, vT_ev, v_d, vals_d = (sem(n) for n in ("vT_d", "vT_ev", "v_d", "vals_d"))
        score_d, max_d, sub_d, exp_d = (sem(n) for n in ("score_d", "max_d", "sub_d", "exp_d"))
        probT_d, probT_ev, av_d, rden_d, y_d = (sem(n) for n in ("probT_d", "probT_ev", "av_d", "rden_d", "y_d"))
        yT_d, yT_ev, o_d, xbo_d, x2_d = (sem(n) for n in ("yT_d", "yT_ev", "o_d", "xbo_d", "x2_d"))
        stat2_d, mv2_d, ve2_d, rs2_d, nb2_d, xn2_d = (
            sem(n) for n in ("stat2_d", "mv2_d", "ve2_d", "rs2_d", "nb2_d", "xn2_d"))
        xn2T_d, xn2T_ev, gate_d, lsub_d, lexp_d = (sem(n) for n in ("xn2T_d", "xn2T_ev", "gate_d", "lsub_d", "lexp_d"))
        route, weight_d, taken_d, earlier_d, rank_d, place, rec_free, rec_d, recw_d, slot_d, disp_out = (
            sem(n) for n in ("route", "weight_d", "taken_d", "earlier_d", "rank_d", "place", "rec_free", "rec_d", "recw_d", "slot_d",
                             "disp_out"))
        w1_in = [sem(f"w1_in{i}") for i in range(2)]
        w2_in = [sem(f"w2_in{i}") for i in range(2)]
        xg_in = [sem(f"xg_in{i}") for i in range(2)]
        xgT_d, xgT_ev, up_d, hid_a, hid_v = (sem(n) for n in ("xgT_d", "xgT_ev", "up_d", "hid_a", "hid_v"))
        down_d, wgt_d, far_d, dst_d, obias_d, ow_d = (
            sem(n) for n in ("down_d", "wgt_d", "far_d", "dst_d", "obias_d", "ow_d"))
        comb_out = [sem(f"comb_out{i}") for i in range(2)]
        chosen_in = [sem(f"chosen_in{c}") for c in range(len(CHUNKS))]
        sum_step, out_d, out_out = (sem(n) for n in ("sum_step", "out_d", "out_out"))

        block = stack.enter_context(nc.Block())

        def pipeline(eng, it):
            first, last = 2, GROUPS - 3
            for g in range(-3, first):
                it(g, g)
            with eng.Fori(first, last) as g:
                it(g, first)
            for g in range(last, GROUPS + 2):
                it(g, g)

        def stages(s):
            return (s + 3 < GROUPS, 0 <= s + 2 < GROUPS, 0 <= s + 1 < GROUPS, 0 <= s < GROUPS,
                    0 <= s - 1 < GROUPS, 0 <= s - 2)

        xv = x.rearrange("(n j) q d -> j q n d", j=2)
        ctx_batches = ctx_d.rearrange("n j k d -> (n j) k d")
        ctx_tiles = ctx_d.rearrange("n j k d -> (j k) n d")
        maskv = mask.rearrange("(n j) q k -> j q n k", j=2)
        slots_v = slots_d.rearrange("(e t p) r -> e p t r", t=SLOT_TILES, p=SLOT_TILE)
        outv = out.rearrange("(n j) q d -> j q n d", j=2)
        choice_v = choice_d.rearrange("(n k p) d -> p n k d", k=TOP_K, p=128)
        w1v = w1
        w2v = w2.rearrange("e (f p) d -> e p f d", p=128)

        @block.sync
        def _(sp):
            sp.dma_start(ctx_batches[:, 0:S, :], ctx[:, 0:S, :]).then_inc(copy_out, 16)
            sp.wait_ge(cleared, 1)
            for j in range(2):
                sp.dma_start(m8[PAD * j:PAD * j + S, :, :], maskv[j, :, :, 0:S]).then_inc(mask_in, 16)
            sp.wait_ge(cleared, 2)
            for j in range(2):
                sp.dma_start(xs[PAD * j:PAD * j + S, :, :], xv[j]).then_inc(x_in, 16)
            for to, frm in ((wq_s, wq), (wk_s, wk)):
                sp.dma_start(to[:], frm).then_inc(w_in, 16)
            sp.dma_start(bq_s[:], bq.rearrange("(p o) -> p o", o=1)).then_inc(w_in, 16)
            sp.dma_start(bk_s[:], bk.rearrange("(p o) -> p o", o=1)).then_inc(w_in, 16)
            sp.wait_ge(cleared, 3)
            sp.dma_start(ctx_batches[:, KEYS:PAD, :], pad_keys[:]
                         .rearrange("b (k d) -> b k d", d=D)).then_inc(copy_out, 16)
            sp.wait_ge(mean_out, 16)
            sp.wait_ge(copy_out, 32)

            def load_context(tile, signal, t):
                sp.dma_start(tile[:], ctx_tiles[:, bass.ds(GP * t, GP), :]).then_inc(signal, 16)

            load_context(ctxk, ctxk_in, 0)
            load_context(ctxv, ctxv_in, 0)
            sp.dma_start(bo_s[:], bo.partition_broadcast(128)).then_inc(bo_in, 16)
            for to, frm in ((wv_s, wv), (wo_s, wo), (gw_s, gate_w)):
                sp.dma_start(to[:], frm).then_inc(wl_in, 16)
            for to, frm in ((bv_s, bv), (gb_s, gate_b)):
                sp.dma_start(to[:], frm.partition_broadcast(128)).then_inc(wl_in, 16)

            def load_rest():
                sp.dma_start(b1_s[:], b1).then_inc(wb_in, 16)
                sp.dma_start(b2_s[:], b2.rearrange("e d -> (e d)").partition_broadcast(128)
                             .rearrange("p (e d) -> p e d", e=E)).then_inc(wb_in, 16)
                for i in range(2):
                    sp.dma_start(w1_s[i][:], w1v[i]).then_inc(w1_in[i], 16)
                    sp.dma_start(w2_s[i][:], w2v[i]).then_inc(w2_in[i], 16)
                sp.dma_start(slots_d.rearrange("(p a) r -> p (a r)", p=SLOT_TILE),
                             zeros[0:SLOT_TILE, 0:E * SLOT_TILES * REC]).then_inc(zero_out, 16)
                sp.dma_start(choice_d.rearrange("(p a) r -> p (a r)", p=128), zeros).then_inc(zero_out, 16)

            def it(g, s):
                norm, front, values, attn, router, dispatch = stages(s)
                if norm and s > -3:
                    wait(sp, frontT_d, g + 3)
                    load_context(ctxk, ctxk_in, g + 3)
                if values:
                    wait(sp, score_d, 4 * g + 4)
                    sp.wait_ge(parts_out, 16 * STACK_WRITES * (g + 2))
                    for to, which in ((q6, 0), (k6, 1)):
                        sp.dma_start(to[:], stacks_d[g + 1, which].rearrange("s (d h) t -> (s d) h t", h=H))\
                            .then_inc(stacks_in, 16)
                if values and s + 2 < GROUPS:
                    sp.wait_ge(vT_d, g + 2)
                    load_context(ctxv, ctxv_in, g + 2)
                if s == -1:
                    sp.wait_ge(all_clear, 1)
                    load_rest()
                if front:
                    sp.wait_ge(lo_d, g + 3)
                    to = stacks_d[g + 2].rearrange("w s c t -> w c s t")
                    for a in range(2):
                        sp.dma_start(to[0, :, 2 * a:2 * a + 2, :], parts[:, 0, a:a + 1, :].broadcast_to([D, 2, GT]))\
                            .then_inc(parts_out, 16)
                        sp.dma_start(to[1, :, 2 * a:2 * a + 2, :], parts[:, 1, 0:2, :]).then_inc(parts_out, 16)
                    sp.dma_start(to[0, :, 4:6, :], parts[:, 0, 0:3:2, :]).then_inc(parts_out, 16)
                    for slot, part in ((4, 2), (5, 0)):
                        sp.dma_start(to[1, :, slot, :], parts[:, 1, part, :]).then_inc(parts_out, 16)

            pipeline(sp, it)

            def load_slots(e, i, first):
                if not first:
                    sp.wait_ge(xgT_d, e - 1)
                    sp.wait_ge(dst_d, e - 1)
                sp.dma_start(xg[i][:], slots_v[e]).then_inc(xg_in[i], 16)

            def load_weights(e, i):
                sp.wait_ge(up_d, FC * (e - 1))
                sp.dma_start(w1_s[i][:], w1v[e]).then_inc(w1_in[i], 16)
                sp.wait_ge(down_d, e - 1)
                sp.dma_start(w2_s[i][:], w2v[e]).then_inc(w2_in[i], 16)

            sp.wait_ge(disp_out, 16 * TOP_K * PAIRS)
            load_slots(0, 0, True)
            load_slots(1, 1, True)
            with sp.Fori(1, E // 2) as two:
                for i in range(2):
                    load_slots(2 * two + i, i, False)
                    load_weights(2 * two + i, i)
            for i in range(2):
                sp.wait_ge(comb_out[i], 16 * SLOT_TILES * E // 2)
            for c, n in enumerate(CHUNKS):
                sp.dma_start(chosen[:, n:n + CHUNK], choice_v[:, n:n + CHUNK]).then_inc(chosen_in[c], 16)
            for c, n in enumerate(CHUNKS):
                sp.wait_ge(out_d, c + 1)
                for j in range(2):
                    sp.dma_start(outv[j, :, n:n + CHUNK, :], x2[PAD * j:PAD * j + S, n:n + CHUNK, :])\
                        .then_inc(out_out, 16)
            sp.wait_ge(out_out, 32 * len(CHUNKS))
            sp.wait_ge(parts_out, 16 * STACK_WRITES * GROUPS)
            sp.wait_ge(zero_out, 32)

        @block.gpsimd
        def _(pool):
            gp = nc.gpsimd
            gp.memset(causal[:], 1.0).then_inc(const_step, 1)
            gp.memset(ident[:], 0.0).then_inc(const_step, 1)
            gp.memset(before[:], 1.0).then_inc(const_step, 1)
            pool.wait_ge(const_step, 3)
            gp.affine_select(out=ident[:], in_=ident[:], compare_op=ALU.not_equal, fill=1.0, base=0,
                             pattern=[[-1, 128]], channel_multiplier=1).then_inc(ident_done, 1)
            gp.affine_select(out=before[:], in_=before[:], compare_op=ALU.is_ge, fill=0.0, base=0,
                             pattern=[[1, 128]], channel_multiplier=-1).then_inc(const_step, 1)
            gp.memset(minus_half[:], -0.5).then_inc(const_step, 1)
            gp.iota(slot_base_i[:], [[SLOTS, E]], base=-1, channel_multiplier=0).then_inc(const_step, 1)
            gp.iota(expert_i[:], [[1, E]], base=0, channel_multiplier=0).then_inc(const_step, 1)
            gp.iota(dest_i[:], [[128, TOP_K], [TOP_K * 128, PAIRS]], base=1, channel_multiplier=1).then_inc(const_step, 1)
            gp.memset(mean[:], 0.0).then_inc(const_step, 1)
            for j in range(2):
                pool.wait_ge(const_step, 9 + j)
                gp.affine_select(out=causal[PAD * j:PAD * (j + 1)], in_=causal[PAD * j:PAD * (j + 1)],
                                 compare_op=ALU.is_ge, fill=0.0, base=0, pattern=[[-1, S]],
                                 channel_multiplier=1).then_inc(const_step, 1)
            pool.wait_ge(const_step, 11)

            pool.wait_ge(flag_done, 1)
            flag = pool.value_load(all_gone[0:1, 0:1], min_val=0, max_val=1)
            with pool.If(flag > 0):
                gp.memset(key_sum[:], 0.0).then_inc(slow_step, 1)
                quarters = ctx.rearrange("b (w c k) d -> (b w) c k d", w=KQ, k=KCH)
                with pool.Fori(0, N_KCH) as c:
                    pool.wait_ge(slow_step, c * KCH + 1)
                    pool.dma_start(keys_c[:], quarters[:, c]).then_inc(slow_dma, 16)
                    pool.wait_ge(slow_dma, c * 16 + 16)
                    hold(pool, passed["pool"])
                    with pool.Fori(0, KCH) as k:
                        pool.wait_ge(slow_step, c * KCH + k + 1)
                        gp.tensor_tensor(key_sum[:], key_sum[:], keys_c[:, k, :], add).then_inc(slow_step, 1)
                pool.wait_ge(slow_step, N_KCH * KCH + 1)
                pool.dma_start(sums_d, key_sum[:]).then_inc(slow_dma, 16)
                pool.wait_ge(slow_dma, 16 * N_KCH + 16)
                pool.dma_start(quarter[:], sums_d.rearrange("(b w) d -> b w d", w=KQ)).then_inc(slow_dma, 16)
                pool.wait_ge(slow_dma, 16 * N_KCH + 32)
                for w in range(KQ):
                    gp.tensor_tensor(mean[:], mean[:], quarter[:, w, :], add).then_inc(slow_step, 1)
                    pool.wait_ge(slow_step, N_KCH * KCH + 2 + w)
                gp.tensor_scalar(mean[:], mean[:], 1.0 / S2, None, mult).then_inc(slow_step, 1)
                pool.wait_ge(slow_step, N_KCH * KCH + 2 + KQ)
            pool.sem_inc(rec_free, 1)
            pool.dma_start(ctx_batches[:, S, :], mean[:]).then_inc(mean_out, 16)

            def it(g, s):
                norm, front, values, attn, router, dispatch = stages(s)
                if router:
                    pool.wait_ge(ve2_d, g)
                    gp.tensor_tensor(rs2[:], ve2[:], minus_half[:], ALU.pow).then_inc(rs2_d, 1)
                if norm:
                    pool.wait_ge(ve1_d, g + 4)
                    wait(pool, xn_d, GP * (g + 3))
                    gp.tensor_tensor(rs1[:], ve1[:], minus_half[:], ALU.pow).then_inc(rs1_d, 1)
                if dispatch:
                    pool.wait_ge(rec_d, 2 * (g - 1))
                    pool.wait_ge(recw_d, g - 1)
                    pool.wait_ge(slot_d, g - 1)
                    hold(pool, passed["pool"])
                    if s == 2:
                        pool.wait_ge(zero_out, 32)
                    for p in range(GP):
                        for k in range(TOP_K):
                            gp.indirect_dma_start(
                                out=slots_d, out_offset=bass.IndirectOffsetOnAxis(ap=slot_i[:, k, p:p + 1], axis=0),
                                in_=rec[:, k, p, :], in_offset=None, bounds_check=E * SLOTS - 1,
                                oob_is_err=False).then_inc(disp_out, 16)
                if front:
                    pool.wait_ge(hi_d, g + 3)
                    gp.tensor_tensor(rest[:], qk[:], parts[:, :, 0, :], sub).then_inc(rest_d, 1)
                if front:
                    pool.wait_ge(mid_d, g + 3)
                    pool.wait_ge(rest_d, g + 3)
                    gp.tensor_tensor(parts[:, :, 2, :], rest[:], parts[:, :, 1, :], sub).then_inc(lo_d, 1)
                if front:
                    if s == -2:
                        pool.wait_ge(x_in, 32)
                        pool.wait_ge(bo_in, 16)
                    t = g + 2
                    gp.tensor_tensor(x2[:, bass.ds(GP * t, GP), :], xs[:, bass.ds(GP * t, GP), :],
                                     bo_s[:].unsqueeze(1).broadcast_to([128, GP, D]), add).then_inc(xbo_d, 1)
                if dispatch:
                    pool.wait_ge(disp_out, 64 * (g - 1))
                    pool.sem_inc(rec_free, 1)

            pipeline(pool, it)

            def send(e, i):
                if isinstance(e, int) and e == 0:
                    pool.wait_ge(zero_out, 16)
                pool.wait_ge(ow_d, e + 1)
                hold(pool, passed["pool"])
                for t in range(SLOT_TILES):
                    gp.indirect_dma_start(
                        out=choice_d, out_offset=bass.IndirectOffsetOnAxis(ap=dst_i[i][:, t:t + 1], axis=0),
                        in_=ow[i][:, t, :], in_offset=None, bounds_check=N_DST - 1,
                        oob_is_err=False).then_inc(comb_out[i], 16)

            send(0, 0)
            send(1, 1)
            with pool.Fori(1, E // 2) as two:
                send(2 * two, 0)
                send(2 * two + 1, 1)

        @block.scalar
        def _(act):
            sc = nc.scalar

            def it(g, s):
                norm, front, values, attn, router, dispatch = stages(s)

                def exponentials(p, i):
                    act.wait_ge(sub_d, 4 * g + 2 * p + i + 1)
                    heads = probs[p][:, 8 * i:8 * i + 8, 0:KEYS]
                    sc.activation(heads, heads, ACT.Exp).then_inc(exp_d, 1)

                def evacuate(p):
                    for i in range(2):
                        act.wait_ge(probT_d, 4 * g + 2 * p + i + 1)
                        sc.activation(probsT[p][:, 4 * i:4 * i + 4, :].rearrange("a h q -> a (h q)"), probT_b[i][:],
                                      ACT.Copy).then_inc(probT_ev, 1)

                def normalise(to, tiles, t, scale, shift, done):
                    for p in range(GP):
                        sc.activation(to[:, p, :], tiles[:, GP * t + p, :], ACT.Identity, bias=shift[:, p:p + 1],
                                      scale=scale[:, p:p + 1]).then_inc(done, 1)

                if router:
                    act.wait_ge(yT_d, g)
                    sc.activation(yT[:], post_p, ACT.Copy).then_inc(yT_ev, 1)
                if dispatch:
                    act.wait_ge(rec_free, g - 1)
                    act.wait_ge(xn2_d, GP * (g - 1))
                    sc.activation(rec[:, :, :, 0:D], xn2[:].unsqueeze(1).broadcast_to([128, TOP_K, GP, D]), ACT.Copy)\
                        .then_inc(rec_d, 1)
                    sc.activation(rec[:, :, :, D + 1], dest[:, :, bass.ds(GP * (g - 2), GP)], ACT.Copy)\
                        .then_inc(rec_d, 1)
                if front:
                    act.wait_ge(frontT_d, g + 3)
                    sc.activation(frontT[:].rearrange("p a t -> p (a t)"), front_b[:], ACT.Copy).then_inc(frontT_ev, 1)
                if attn:
                    exponentials(0, 0)
                    exponentials(0, 1)
                if attn:
                    evacuate(0)
                if attn:
                    exponentials(1, 0)
                    exponentials(1, 1)
                if router:
                    act.wait_ge(nb2_d, g)
                    wait(act, xn2T_d, g - 1)
                    if dispatch:
                        act.wait_ge(rec_d, 2 * (g - 1) - 1)
                    normalise(xn2, x2, g - 1, rs2, nb2, xn2_d)
                if front:
                    if s == -2:
                        act.wait_ge(bqs_done, 1)
                        act.wait_ge(w_in, 64)
                    act.wait_ge(qk_d, g + 3)
                    wait(act, lo_d, g + 2)
                    sc.activation(qk[:, 0, :], front_b[:, 0:GT], ACT.Identity, bias=bqs[:],
                                  scale=float(1.0 / np.sqrt(np.float32(HD)))).then_inc(qk_ev, 1)
                    sc.activation(qk[:, 1, :], front_b[:, GT:2 * GT], ACT.Identity, bias=bk_s[:])\
                        .then_inc(qk_ev, 1)
                    act.wait_ge(qk_ev, 2 * (g + 3))
                    wait(act, parts_out, 16 * STACK_WRITES * (g + 2))
                    sc.activation(parts[:, :, 0, :], qk[:], ACT.Copy).then_inc(hi_d, 1)
                if router:
                    act.wait_ge(xn2T_d, g)
                    sc.activation(xn2T[:], post_p, ACT.Copy).then_inc(xn2T_ev, 1)
                if attn:
                    evacuate(1)
                if values:
                    act.wait_ge(vT_d, g + 2)
                    for n in range(2):
                        sc.activation(ctxvT[:, :, n, :], front_b[:, 0:GT].rearrange("p (b k) -> p b k", k=PAD),
                                      ACT.Copy).then_inc(vT_ev, 1)
                if router:
                    act.wait_ge(lsub_d, g)
                    sc.activation(prob[:], logit[:], ACT.Exp).then_inc(lexp_d, 1)
                if front:
                    act.wait_ge(rest_d, g + 3)
                    sc.activation(parts[:, :, 1, :], rest[:], ACT.Copy).then_inc(mid_d, 1)
                if norm:
                    act.wait_ge(nb1_d, g + 4)
                    wait(act, frontT_d, g + 3)
                    normalise(xn, xs, g + 3, rs1, nb1, xn_d)

            pipeline(act, it)
            act.wait_ge(wb_in, 32)

            def expert(e, i):
                act.wait_ge(xgT_d, e + 1)
                sc.activation(xgT[i][:], probT_b[i][:, 0:SLOTS], ACT.Copy).then_inc(xgT_ev, 1)
                for f in (0, 2):
                    act.wait_ge(up_d, FC * e + f + 1)
                    sc.activation(hid[i][:, f, :], bank[f][:, 0:SLOTS], ACT.Relu, bias=b1_s[:, e, f:f + 1])\
                        .then_inc(hid_a, 1)

            with act.Fori(0, E // 2) as two:
                expert(2 * two, 0)
                expert(2 * two + 1, 1)

        @block.vector
        def _(dve):
            ve = nc.vector

            def constants():
                dve.wait_ge(ident_done, 1)
                ve.tensor_copy(ident_b[:], ident[:]).then_inc(vconst, 1)
                ve.reduce_sum(row_ok[:], ident[:].rearrange("p (j q) -> p j q", j=2)[:, :, 0:S], mybir.AxisListType.XY)\
                    .then_inc(vconst, 1)
                ve.memset(valid[:], 1.0).then_inc(vconst, 1)
                dve.wait_ge(const_step, 9)
                dve.wait_ge(vconst, 3)
                ve.tensor_scalar(before[:], before[:], row_ok[:], None, mult).then_inc(vconst, 1)
                ve.tensor_scalar(valid[:], valid[:], row_ok[:], None, mult).then_inc(vconst, 1)
                ve.tensor_scalar(row_far[:], row_ok[:], -FAR, FAR, mult, add).then_inc(vconst, 1)
                ve.tensor_copy(expert_no[:], expert_i[:]).then_inc(vconst, 1)
                ve.tensor_copy(dest[:], dest_i[:]).then_inc(vconst, 1)
                dve.wait_ge(vconst, 8)
                ve.tensor_scalar(slot_base[:], slot_base_i[:], row_far[:], None, add).then_inc(const_done, 1)

            ve.memset(m8[:].rearrange("p a b -> p (a b)").bitcast(i32), 0).then_inc(cleared, 1)
            ve.memset(xs[:], 0.0).then_inc(cleared, 1)
            ve.memset(pad_keys[:], 0.0).then_inc(cleared, 1)

            def mask_to_bias():
                dve.wait_ge(mask_in, 32)
                dve.wait_ge(const_step, 11)
                ve.tensor_tensor(mc[:], m8[:], causal[:].unsqueeze(1).broadcast_to([128, PAIRS, S]), mult)\
                    .then_inc(bias_step, 1)
                ve.memset(bias[:], GONE).then_inc(bias_step, 1)
                dve.wait_ge(bias_step, 2)
                ve.reduce_max(some[:], mc[:], X).then_inc(bias_step, 1)
                dve.wait_ge(bias_step, 3)
                ve.tensor_scalar(bias[:, :, 0:S], mc[:], -1.0, -GONE, add, mult)
                ve.tensor_scalar(bias[:, :, S], some[:], GONE, None, mult).then_inc(bias_done, 1)
                dve.wait_ge(kept_done, 1)
                ve.reduce_sum(rows_kept[:], mix_b[0:1, 0:PAIRS], X).then_inc(flag_step, 1)
                dve.wait_ge(flag_step, 1)
                ve.tensor_scalar(all_gone[:], rows_kept[:], B * S - 0.5, None, ALU.is_lt).then_inc(flag_done, 1)
            constants()
            mask_to_bias()
            dve.wait_ge(x_in, 32)

            def stats(t, tiles, stat, stat_d):
                for p in range(GP):
                    ve.bn_stats(stat[:, p, :], tiles[:, GP * t + p, :]).then_inc(stat_d, 1)

            def mean_variance(t, stat, mv, stat_d, mv_d):
                wait(dve, stat_d, GP * (t + 1))
                hold(dve, passed["dve"])
                for p in range(GP):
                    ve.bn_aggr(mv[:, p, :], stat[:, p, :]).then_inc(mv_d, 1)

            def add_eps(t, mv, vee, mv_d, ve_d):
                wait(dve, mv_d, GP * (t + 1))
                ve.tensor_scalar(vee[:], mv[:, :, 1], 1e-5, None, add).then_inc(ve_d, 1)

            def shift(t, mv, rs, nb, rs_d, nb_d):
                wait(dve, rs_d, t + 1)
                ve.scalar_tensor_tensor(nb[:], mv[:, :, 0], -1.0, rs[:], mult, mult).then_inc(nb_d, 1)

            def clear_buffers():
                dve.wait_ge(w_in, 64)
                ve.tensor_scalar(bqs[:], bq_s[:], float(1.0 / np.sqrt(np.float32(HD))), None, mult)\
                    .then_inc(bqs_done, 1)
                ve.memset(chosen[:], 0.0).then_inc(all_clear, 1)
                for p in range(GP):
                    ve.memset(probs[p][:], 0.0)
                ve.memset(earlier[:], 0.0).then_inc(cleared, 1)
                ve.memset(vals[:], 0.0).then_inc(cleared, 1)
                dve.wait_ge(cleared, 5)
                ve.memset(vals[0:PAD, :, :, HD], 1.0)
                ve.memset(vals[PAD:128, :, :, VW - 1], 1.0).then_inc(cleared, 1)

            def it(g, s):
                norm, front, values, attn, router, dispatch = stages(s)

                def maxima(p, i):
                    dve.wait_ge(score_d, 4 * g + 2 * p + i + 1)
                    ve.reduce_max(row_max[:, p, 8 * i:8 * i + 8],
                                  score_b[p][i][:].rearrange("q (h k) -> q h k", k=PAD)[:, :, 0:KEYS], X)\
                        .then_inc(max_d, 1)

                def less_maxima(p, i):
                    if i == 0:
                        wait(dve, probT_d, 4 * (g - 1) + 2 * p + 2)
                    dve.wait_ge(max_d, 4 * g + 2 * p + i + 1)
                    ve.tensor_tensor(probs[p][:, 8 * i:8 * i + 8, 0:KEYS],
                                     score_b[p][i][:].rearrange("q (h k) -> q h k", k=PAD)[:, :, 0:KEYS],
                                     row_max[:, p, 8 * i:8 * i + 8].unsqueeze(2).broadcast_to([128, 8, KEYS]), sub)\
                        .then_inc(sub_d, 1)

                def divide(p, t):
                    dve.wait_ge(av_d, 2 * t + p + 1)
                    heads = av_p.rearrange("q (h d) -> q h d", d=HD + 1)
                    ve.reciprocal(rden[:, p, :], heads[:, :, HD]).then_inc(rden_d, 1)
                    dve.wait_ge(rden_d, 2 * t + p + 1)
                    ve.tensor_tensor(y[:, p, :].rearrange("q (h d) -> q h d", d=HD), heads[:, :, 0:HD],
                                     rden[:, p, :].unsqueeze(2).broadcast_to([128, H, HD]), mult).then_inc(y_d, 1)

                def values_in(j):
                    if s == -1 and j == 0:
                        dve.wait_ge(wl_in, 80)
                        dve.wait_ge(cleared, 6)
                    dve.wait_ge(v_d, g + 2)
                    wait(dve, av_d, 2 * (g + 1))
                    half = slice(PAD * j, PAD * (j + 1))
                    ve.tensor_tensor(
                        vals[half, :, :, (HD + 1) * j:(HD + 1) * j + HD],
                        front_b[half, :].rearrange("k (b h two d) -> k b h two d", b=2 * GP, two=2, d=HD)[:, :, :, j, :],
                        bv_s[half, :].rearrange("k (h two d) -> k h two d", two=2, d=HD)[:, :, j, :]
                        .unsqueeze(1).broadcast_to([PAD, 2 * GP, HP, HD]), add).then_inc(vals_d, 1)

                def per_tile(ap):
                    return ap.unsqueeze(2).broadcast_to([128, GP, E])

                def ranks():
                    t = g - 2
                    dve.wait_ge(rank_d, t + 1)
                    rank = rank_p.rearrange("q (p e) -> q p e", e=E)
                    ve.tensor_scalar(over[:], rank, CAP + 0.5, FAR, ALU.is_gt, mult).then_inc(place, 1)
                    ve.tensor_tensor(slot_e[:], rank, slot_base[:].unsqueeze(1).broadcast_to([128, GP, E]), add)\
                        .then_inc(place, 1)
                    ve.tensor_tensor(earlier[:, 0, :], earlier[:, 1, :], taken[:, 1, :], add).then_inc(earlier_d, 1)

                def slots_of_experts():
                    dve.wait_ge(place, 4 * (g - 2) + 2)
                    ve.tensor_tensor(slot_e[:], slot_e[:], over[:], add).then_inc(place, 1)

                def slots_of_choices():
                    dve.wait_ge(place, 4 * (g - 2) + 3)
                    ve.tensor_tensor(slot_k[:], onehot[:], slot_e[:].unsqueeze(1)
                                     .broadcast_to([128, TOP_K, GP, E]), mult).then_inc(place, 1)

                def slots():
                    dve.wait_ge(place, 4 * (g - 1))
                    dve.wait_ge(rec_free, g - 1)
                    dve.wait_ge(weight_d, g - 1)
                    ve.tensor_copy(rec[:, :, :, D], weight[:]).then_inc(recw_d, 1)
                    with nc.allow_low_precision(reason="slots are whole numbers, summed in float32"):
                        ve.reduce_sum(slot_i[:], slot_k[:], X).then_inc(slot_d, 1)

                def residual():
                    dve.wait_ge(o_d, g)
                    dve.wait_ge(xbo_d, g)
                    tiles = x2[:, bass.ds(GP * (g - 1), GP), :].rearrange("q p d -> q (p d)")
                    ve.tensor_tensor(tiles, tiles, post_p, add).then_inc(x2_d, 1)

                def step(ins):
                    ins.then_inc(route, 1)

                def after(t, steps):
                    dve.wait_ge(route, ROUTE * t + steps)

                def logits(t):
                    dve.wait_ge(gate_d, t + 1)
                    step(ve.tensor_tensor(logit[:], gate_p.rearrange("q (p e) -> q p e", e=E),
                                          gb_s[:].unsqueeze(1).broadcast_to([128, GP, E]), add))
                    after(t, 1)
                    step(ve.reduce_max(lmax[:], logit[:], X))
                    after(t, 2)
                    ve.tensor_tensor(logit[:], logit[:], per_tile(lmax[:]), sub).then_inc(lsub_d, 1)

                def experts_probs(t):
                    dve.wait_ge(lexp_d, t + 1)
                    step(ve.reduce_sum(esum[:], prob[:], X))
                    after(t, 3)
                    step(ve.reciprocal(esum[:], esum[:]))
                    after(t, 4)
                    step(ve.tensor_tensor(prob[:], prob[:], per_tile(esum[:]), mult))
                    after(t, 5)
                    hold(dve, passed["dve"])
                    for p in range(GP):
                        step(ve.max(top[:, p, :], prob[:, p, :]))

                def two_greatest(t):
                    after(t, 5 + GP)
                    hold(dve, passed["dve"])
                    for p in range(GP):
                        step(ve.max_index(top_i[:, p, :], top[:, p, :], prob[:, p, :]))
                    step(ve.tensor_tensor(topsum[:], top[:, :, 0], top[:, :, 1], add))

                def choices(t):
                    after(t, 6 + 2 * GP)
                    step(ve.tensor_tensor(onehot[:], expert_no[:].unsqueeze(1).unsqueeze(1)
                                          .broadcast_to([128, TOP_K, GP, E]),
                                          top_i[:, :, 0:TOP_K].rearrange("q p k -> q k p").unsqueeze(3)
                                          .broadcast_to([128, TOP_K, GP, E]), ALU.is_equal))
                    step(ve.reciprocal(topsum[:], topsum[:]))

                def weights(t):
                    after(t, 8 + 2 * GP)
                    ve.tensor_tensor(taken[:], onehot[:, 0], onehot[:, 1], add).then_inc(taken_d, 1)
                    ve.tensor_tensor(weight[:], top[:, :, 0:TOP_K].rearrange("q p k -> q k p"),
                                     topsum[:].unsqueeze(1).broadcast_to([128, TOP_K, GP]), mult).then_inc(weight_d, 1)

                def add_earlier(t):
                    dve.wait_ge(taken_d, t + 1)
                    wait(dve, earlier_d, 2 * t)
                    ve.tensor_tensor(earlier[:, 1, :], earlier[:, 0, :], taken[:, 0, :], add).then_inc(earlier_d, 1)

                if s == -2:
                    clear_buffers()
                if attn:
                    maxima(0, 0)
                if dispatch:
                    two_greatest(g - 2)
                if attn:
                    less_maxima(0, 0)
                if dispatch:
                    choices(g - 2)
                if attn:
                    maxima(0, 1)
                if dispatch:
                    weights(g - 2)
                if attn:
                    less_maxima(0, 1)
                if dispatch:
                    add_earlier(g - 2)
                if router:
                    residual()
                if attn:
                    maxima(1, 0)
                if router:
                    dve.wait_ge(x2_d, g)
                    hold(dve, passed["dve"])
                    stats(g - 1, x2, stat2, stat2_d)
                if norm:
                    stats(g + 3, xs, stat1, stat1_d)
                if dispatch:
                    ranks()
                if router:
                    mean_variance(g - 1, stat2, mv2, stat2_d, mv2_d)
                if norm:
                    mean_variance(g + 3, stat1, mv1, stat1_d, mv1_d)
                if dispatch:
                    slots_of_experts()
                if router:
                    add_eps(g - 1, mv2, ve2, mv2_d, ve2_d)
                if norm:
                    add_eps(g + 3, mv1, ve1, mv1_d, ve1_d)
                if attn:
                    less_maxima(1, 0)
                if dispatch:
                    slots_of_choices()
                if attn:
                    maxima(1, 1)
                if dispatch:
                    slots()
                if router:
                    shift(g - 1, mv2, rs2, nb2, rs2_d, nb2_d)
                if attn:
                    less_maxima(1, 1)
                if norm:
                    shift(g + 3, mv1, rs1, nb1, rs1_d, nb1_d)
                if attn:
                    divide(0, g)
                if router:
                    logits(g - 1)
                    experts_probs(g - 1)
                if attn:
                    divide(1, g)
                if values:
                    values_in(0)
                    values_in(1)

            ROUTE = 12
            pipeline(dve, it)

            def expert(e, i, first=False):
                for f in (1, 3):
                    dve.wait_ge(up_d, FC * e + f + 1)
                    ve.tensor_scalar(hid[i][:, f, :], bank[f][:, 0:SLOTS], b1_s[:, e, f:f + 1], 0.0, add, ALU.max)\
                        .then_inc(hid_v, 1)
                dve.wait_ge(xg_in[i], 8 * (e - i) + 16)
                if not first:
                    dve.wait_ge(comb_out[i], 8 * SLOT_TILES * (e - i))
                ve.tensor_copy(weight_s[i][:], xg[i][:, :, D]).then_inc(wgt_d, 1)
                ve.tensor_scalar(far_s[i][:], xg[i][:, :, D + 1], 0.5, FAR, ALU.is_lt, mult).then_inc(far_d, 1)
                dve.wait_ge(far_d, e + 1)
                ve.scalar_tensor_tensor(dst_i[i][:], xg[i][:, :, D + 1], -1.0, far_s[i][:], add, add).then_inc(dst_d, 1)
                dve.wait_ge(down_d, e + 1)
                if not first:
                    dve.wait_ge(ow_d, e - 1)
                ve.tensor_tensor(obias[:], bank[6 + i][0:SLOT_TILE, 0:SLOT_TILES * D].rearrange("s (t d) -> s t d", d=D),
                                 b2_s[0:SLOT_TILE, e, :].unsqueeze(1).broadcast_to([SLOT_TILE, SLOT_TILES, D]), add)\
                    .then_inc(obias_d, 1)
                dve.wait_ge(obias_d, e + 1)
                dve.wait_ge(wgt_d, e + 1)
                ve.tensor_tensor(ow[i][:], obias[:],
                                 weight_s[i][:].unsqueeze(2).broadcast_to([SLOT_TILE, SLOT_TILES, D]), mult)\
                    .then_inc(ow_d, 1)

            dve.wait_ge(wb_in, 32)
            expert(0, 0, first=True)
            expert(1, 1, first=True)
            with dve.Fori(1, E // 2) as two:
                expert(2 * two, 0)
                expert(2 * two + 1, 1)
            dve.wait_ge(dst_d, E)
            for c, n in enumerate(CHUNKS):
                dve.wait_ge(chosen_in[c], 16)
                tiles = x2[:, n:n + CHUNK, :]
                ve.tensor_tensor(tiles, tiles, chosen[:, n:n + CHUNK, 0, :], add).then_inc(sum_step, 1)
                dve.wait_ge(sum_step, c + 1)
                ve.tensor_tensor(tiles, tiles, chosen[:, n:n + CHUNK, 1, :], add).then_inc(out_d, 1)

        @block.tensor
        def _(pe):
            mm, tr = nc.tensor.matmul, nc.tensor.transpose
            pe.wait_ge(const_done, 1)
            pe.wait_ge(bias_step, 3)
            mm(mix_b[0:1, 0:PAIRS], valid[:, 0:1], some[:], start=True, stop=True).then_inc(kept_done, 1)

            def it(g, s):
                norm, front, values, attn, router, dispatch = stages(s)

                def scores(p, i):
                    wait(pe, sub_d, 4 * g + ((0, -2), (-1, 1))[p][i])
                    rows = bias[:, GP * g + p, :].unsqueeze(1).broadcast_to([128, 8, PAD])
                    mm(score_b[p][i][:], ident_b[:], rows, start=True, stop=False, skip_group_check=True)
                    for h in range(8):
                        for j in range(2):
                            cols = slice(128 * p + PAD * j, 128 * p + PAD * (j + 1))
                            last = mm(score_b[p][i][PAD * j:PAD * (j + 1), PAD * h:PAD * (h + 1)],
                                      q6[:, 8 * i + h, cols], k6[:, 8 * i + h, cols], start=False, stop=True,
                                      skip_group_check=True)
                    last.then_inc(score_d, 1)

                def transpose_probs(p):
                    for i in range(2):
                        pe.wait_ge(exp_d, 4 * g + 2 * p + i + 1)
                        wait(pe, probT_ev, 4 * g + 2 * p + i - 1)
                        for h in range(4):
                            hp = 4 * i + h
                            last = tr(probT_b[i][:, 128 * h:128 * (h + 1)],
                                      probs[p][:, 2 * hp:2 * hp + 2, :].rearrange("q h k -> q (h k)"), ident[:])
                        last.then_inc(probT_d, 1)

                def mix_values(p):
                    pe.wait_ge(probT_ev, 4 * g + 2 * p + 2)
                    pe.wait_ge(vals_d, 2 * (g + 1))
                    wait(pe, y_d, 2 * g + p)
                    if dispatch:
                        pe.wait_ge(place, 4 * (g - 2) + 2)
                    for j in range(2):
                        for hp in range(HP):
                            last = mm(av_p[PAD * j:PAD * (j + 1), VW * hp:VW * (hp + 1)],
                                      probsT[p][:, hp, PAD * j:PAD * (j + 1)], vals[:, GP * p + j, hp, :],
                                      start=True, stop=True, skip_group_check=True)
                    last.then_inc(av_d, 1)

                if s == -2:
                    pe.wait_ge(w_in, 64)
                def transpose_to_post(tile):
                    for p in range(GP):
                        last = tr(post_p[:, 128 * p:128 * (p + 1)], tile[:, p, :], ident[:])
                    return last

                if attn:
                    if s == 0:
                        pe.wait_ge(bias_done, 1)
                        pe.wait_ge(cleared, 6)
                    pe.wait_ge(stacks_in, 32 * (g + 1))
                    scores(0, 0)
                if router:
                    pe.wait_ge(y_d, 2 * g)
                    transpose_to_post(y).then_inc(yT_d, 1)
                if attn:
                    scores(0, 1)
                if front:
                    pe.wait_ge(xn_d, GP * (g + 3))
                    pe.wait_ge(ctxk_in, 16 * (g + 3))
                    wait(pe, vals_d, 2 * (g + 1))
                    for p in range(GP):
                        tr(front_b[:, 128 * p:128 * (p + 1)], xn[:, p, :], ident[:])
                        last = tr(front_b[:, GT + 128 * p:GT + 128 * (p + 1)], ctxk[:, p, :], ident[:])
                    last.then_inc(frontT_d, 1)
                if attn:
                    scores(1, 0)
                if router:
                    if s == 1:
                        pe.wait_ge(wl_in, 80)
                    pe.wait_ge(yT_ev, g)
                    for p in range(GP):
                        last = mm(post_p[:, 128 * p:128 * (p + 1)], yT[:, 128 * p:128 * (p + 1)], wo_s[:],
                                  start=True, stop=True)
                    last.then_inc(o_d, 1)
                if attn:
                    scores(1, 1)
                if dispatch:
                    pe.wait_ge(earlier_d, 2 * (g - 2) + 1)
                    pe.wait_ge(y_d, 2 * g if attn else 2 * GROUPS)
                    mm(rank_p, before[:], taken[:].rearrange("q p e -> q (p e)"), start=True, stop=False)
                    mm(rank_p, valid[:], earlier[:].rearrange("q p e -> q (p e)"), start=False, stop=True)\
                        .then_inc(rank_d, 1)
                if attn:
                    transpose_probs(0)
                if front:
                    pe.wait_ge(frontT_ev, g + 3)
                    mm(front_b[:, 0:GT], wq_s[:], frontT[:, 0, :], start=True, stop=True)
                    mm(front_b[:, GT:2 * GT], wk_s[:], frontT[:, 1, :], start=True, stop=True).then_inc(qk_d, 1)
                if attn:
                    mix_values(0)
                if router:
                    pe.wait_ge(xn2_d, GP * g)
                    transpose_to_post(xn2).then_inc(xn2T_d, 1)
                if attn:
                    transpose_probs(1)
                if values:
                    if front:
                        pe.wait_ge(qk_ev, 2 * (g + 3))
                    else:
                        wait(pe, vals_d, 2 * (g + 1))
                    pe.wait_ge(ctxv_in, 16 * (g + 2))
                    for p in range(GP):
                        last = tr(front_b[:, 128 * p:128 * (p + 1)], ctxv[:, p, :], ident[:])
                    last.then_inc(vT_d, 1)
                if router:
                    pe.wait_ge(xn2T_ev, g)
                    for p in range(GP):
                        last = mm(gate_p[:, E * p:E * (p + 1)], xn2T[:, 128 * p:128 * (p + 1)], gw_s[:],
                                  start=True, stop=True)
                    last.then_inc(gate_d, 1)
                if attn:
                    mix_values(1)
                if values:
                    if s == -1:
                        pe.wait_ge(wl_in, 80)
                    pe.wait_ge(vT_ev, 2 * (g + 2))
                    for b in range(2 * GP):
                        last = mm(front_b[:, D * b:D * (b + 1)], ctxvT[:, b, :, :].rearrange("c n k -> c (n k)"),
                                  wv_s[:], start=True, stop=True)
                    last.then_inc(v_d, 1)

            pipeline(pe, it)

            def transpose_slots(e, i):
                pe.wait_ge(xg_in[i], 8 * (e - i) + 16)
                wait(pe, xgT_ev, e - 1)
                for t in range(SLOT_TILES):
                    last = tr(probT_b[i][:, SLOT_TILE * t:SLOT_TILE * (t + 1)], xg[i][:, t, 0:D],
                              ident[0:SLOT_TILE, 0:SLOT_TILE])
                last.then_inc(xgT_d, 1)

            def expert(e, i, more):
                pe.wait_ge(w1_in[i], 8 * (e - i) + 16)
                pe.wait_ge(xgT_ev, e + 1)
                wait(pe, hid_a, 2 * e)
                wait(pe, hid_v, 2 * e)
                for f in range(FC):
                    mm(bank[f][:, 0:SLOTS], w1_s[i][:, 128 * f:128 * (f + 1)], xgT[i][:], start=True, stop=True)\
                        .then_inc(up_d, 1)
                if more:
                    transpose_slots(e + 1, 1 - i)
                pe.wait_ge(w2_in[i], 8 * (e - i) + 16)
                wait(pe, obias_d, e - 1)
                for f in range(FC):
                    pe.wait_ge(hid_v if f % 2 else hid_a, 2 * e + 1 + f // 2)
                    for t in range(SLOT_TILES):
                        last = mm(bank[6 + i][0:SLOT_TILE, D * t:D * (t + 1)],
                                  hid[i][:, f, SLOT_TILE * t:SLOT_TILE * (t + 1)], w2_s[i][:, f, :],
                                  start=(f == 0 and t == 0), stop=(f == FC - 1), skip_group_check=True)
                last.then_inc(down_d, 1)

            transpose_slots(0, 0)
            expert(0, 0, True)
            expert(1, 1, True)
            with pe.Fori(1, E // 2 - 1) as two:
                expert(2 * two, 0, True)
                expert(2 * two + 1, 1, True)
            expert(E - 2, 0, True)
            expert(E - 1, 1, False)


def kernel(x, ctx_1024, mask_BxSxS2_bf1, L0_xattn_Wk, L0_xattn_bk, L0_xattn_Wq, L0_xattn_bq, L0_xattn_Wv,
           L0_xattn_bv, L0_xattn_Wo, L0_xattn_bo, L0_ffn_gate_w, L0_ffn_gate_b, L0_ffn_w1, L0_ffn_b1,
           L0_ffn_w2, L0_ffn_b2):
    import concourse.bacc as bacc
    from concourse.bass_utils import run_bass_kernel_spmd

    def by_feature(a):
        a = np.asarray(a)
        return np.ascontiguousarray(a.reshape(*a.shape[:-1], H, HD).swapaxes(-1, -2).reshape(a.shape))

    arrays = {
        "x": np.asarray(x), "ctx": np.asarray(ctx_1024), "mask": np.asarray(mask_BxSxS2_bf1).view(np.uint8),
        "wk": by_feature(L0_xattn_Wk), "bk": by_feature(L0_xattn_bk),
        "wq": by_feature(L0_xattn_Wq), "bq": by_feature(L0_xattn_bq),
        "wv": np.asarray(L0_xattn_Wv), "bv": np.asarray(L0_xattn_bv),
        "wo": np.asarray(L0_xattn_Wo), "bo": np.asarray(L0_xattn_bo),
        "gate_w": np.asarray(L0_ffn_gate_w), "gate_b": np.asarray(L0_ffn_gate_b),
        "w1": np.asarray(L0_ffn_w1),
        "b1": np.ascontiguousarray(np.asarray(L0_ffn_b1).reshape(E, FC, 128).transpose(2, 0, 1)),
        "w2": np.asarray(L0_ffn_w2), "b2": np.asarray(L0_ffn_b2),
    }
    nc = bacc.Bacc("TRN2", target_bir_lowering=False, num_devices=1)
    ins, feed = [], {}
    for name, a in arrays.items():
        a = np.ascontiguousarray(a)
        feed[f"{name}_in"] = a
        ins.append(nc.dram_tensor(f"{name}_in", a.shape, mybir.dt.from_np(a.dtype), kind="ExternalInput").ap())
    out = nc.dram_tensor("out", (B, S, D), mybir.dt.float32, kind="ExternalOutput").ap()
    build(nc, *ins, out)
    return run_bass_kernel_spmd(nc, [feed], core_ids=[0]).results[0]["out"]
```

```python
from contextlib import ExitStack

import numpy as np

import concourse.bass as bass
from concourse import mybir

B, S, S2, D = 32, 56, 1500, 128
H, HD = 16, 8
E, FF, TOP_K = 8, 512, 2
CAP = int(1.25 * B * S / E)
SLOT_TILES = 3
SLOT_TILE = -(-CAP // SLOT_TILES)
SLOTS = SLOT_TILE * SLOT_TILES
PAD = 64
PAIRS = B // 2
GP = 2
GROUPS = PAIRS // GP
GT = GP * 2 * PAD
KEYS = S + 1
HP = H // 2
VW = 2 * (HD + 1)
FC = FF // 128
REC = D + 2
N_DST = PAIRS * TOP_K * 128
FAR = 8192.0
GONE = -1.0e30
PRODUCTS = 6
STACK_WRITES = 7
CHUNKS = [(n, 4) for n in range(0, PAIRS, 4)]
KQ = 4
KCH = 25
N_KCH = S2 // KQ // KCH


def wait(eng, sem, value):
    if isinstance(value, int) and value <= 0:
        return
    eng.wait_ge(sem, value)


def hold(eng, passed):
    eng.sem_inc(passed, 1)


def build(nc, x, ctx, mask, wk, bk, wq, bq, wv, bv, wo, bo, gate_w, gate_b, w1, b1, w2, b2, out):
    f32, bf16, i32, u8 = mybir.dt.float32, mybir.dt.bfloat16, mybir.dt.int32, mybir.dt.uint8
    ALU, ACT, X = mybir.AluOpType, mybir.ActivationFunctionType, mybir.AxisListType.X
    add, sub, mult = ALU.add, ALU.subtract, ALU.mult

    with ExitStack() as stack:
        def sb(name, shape, dt=f32):
            return stack.enter_context(nc.sbuf_tensor(name, shape, dt))

        def sem(name):
            return stack.enter_context(nc.semaphore(name))

        def dram(name, shape, dt=f32):
            return nc.dram_tensor(name, shape, dt, kind="Internal").ap()

        stacks_d = dram("stacks_d", (GROUPS, 2, PRODUCTS, D, GT), bf16)
        slots_d = dram("slots_d", (E * SLOTS, REC))
        choice_d = dram("choice_d", (N_DST, D))
        sums_d = dram("sums_d", (KQ * B, D))

        ident = sb("ident", [128, 128])
        ident_b = sb("ident_b", [128, 128], bf16)
        causal = sb("causal", [128, S], bf16)
        before = sb("before", [128, 128], bf16)
        valid = sb("valid", [128, 128], bf16)
        slot_base_i = sb("slot_base_i", [128, E], i32)
        slot_base = sb("slot_base", [128, E])
        expert_i = sb("expert_i", [128, E], i32)
        expert_no = sb("expert_no", [128, E])
        dest_i = sb("dest_i", [128, TOP_K, PAIRS], i32)
        dest = sb("dest", [128, TOP_K, PAIRS])
        row_ok, row_far = sb("row_ok", [128, 1]), sb("row_far", [128, 1])
        minus_half = sb("minus_half", [128, GP])
        wq_s, wk_s, wv_s, wo_s = (sb(n, [128, D]) for n in ("wq_s", "wk_s", "wv_s", "wo_s"))
        bq_s, bk_s, bv_s, bqs = (sb(n, [128, 1]) for n in ("bq_s", "bk_s", "bv_s", "bqs"))
        bo_s = sb("bo_s", [128, D])
        gw_s, gb_s = sb("gw_s", [128, E]), sb("gb_s", [128, E])
        b1_s = sb("b1_s", [128, E, FC])
        b2_s = sb("b2_s", [128, E, D])
        xs = sb("xs", [128, PAIRS, D])
        x2 = sb("x2", [128, PAIRS, D])
        m8 = sb("m8", [128, PAIRS, S], u8)
        mc = sb("mc", [128, PAIRS, S], bf16)
        some = sb("some", [128, PAIRS], bf16)
        bias = sb("bias", [128, PAIRS, PAD], bf16)
        rows_kept = sb("rows_kept", [1, 1])
        all_gone = sb("all_gone", [1, 1], i32)

        key_sum = sb("key_sum", [128, D])
        keys_c = sb("keys_c", [128, KCH, D])
        quarter = sb("quarter", [B, KQ, D])
        mean = sb("mean", [B, D])
        meanT = sb("meanT", [128, B])

        ctxk = sb("ctxk", [128, GP, D])
        stat1, mv1 = sb("stat1", [128, GP, 6]), sb("mv1", [128, GP, 2])
        ve1, rs1, nb1 = (sb(n, [128, GP]) for n in ("ve1", "rs1", "nb1"))
        xn = sb("xn", [128, GP, D])
        frontT = sb("frontT", [128, 2, GT])
        qk = sb("qk", [128, 2, GT])
        rest = sb("rest", [128, 2, GT])
        parts = sb("parts", [128, 2, 3, GT], bf16)
        ctxvT = sb("ctxvT", [128, 2 * GP, 2, PAD])
        vals = sb("vals", [128, 2 * GP, HP, VW])

        q6 = sb("q6", [PRODUCTS * HD, H, GT], bf16)
        k6 = sb("k6", [PRODUCTS * HD, H, GT], bf16)
        row_max = sb("row_max", [128, GP, H])
        probs = [sb(f"probs{p}", [128, H, PAD]) for p in range(GP)]
        probsT = [sb(f"probsT{p}", [128, HP, 128]) for p in range(GP)]
        rden = sb("rden", [128, GP, H])
        y = sb("y", [128, GP, D])
        yT = sb("yT", [128, GT])

        stat2, mv2 = sb("stat2", [128, GP, 6]), sb("mv2", [128, GP, 2])
        ve2, rs2, nb2 = (sb(n, [128, GP]) for n in ("ve2", "rs2", "nb2"))
        xn2 = sb("xn2", [128, GP, D])
        rec = sb("rec", [128, TOP_K, GP, REC])
        xn2T = sb("xn2T", [128, GT])
        logit = sb("logit", [128, GP, E])
        lmax = sb("lmax", [128, GP])
        prob = sb("prob", [128, GP, E])
        esum = sb("esum", [128, GP])
        top = sb("top", [128, GP, E])
        top_i = sb("top_i", [128, GP, E], mybir.dt.uint32)
        weight = sb("weight", [128, TOP_K, GP])
        onehot = sb("onehot", [128, TOP_K, GP, E])
        topsum = sb("topsum", [128, GP])
        taken = sb("taken", [128, GP, E], bf16)
        earlier = sb("earlier", [128, GP, E], bf16)
        over = sb("over", [128, GP, E])
        slot_e = sb("slot_e", [128, GP, E])
        slot_k = sb("slot_k", [128, TOP_K, GP, E])
        slot_i = sb("slot_i", [128, TOP_K, GP], i32)

        w1_s = [sb(f"w1_s{i}", [128, FF]) for i in range(2)]
        w2_s = [sb(f"w2_s{i}", [128, FC, D]) for i in range(2)]
        xg = [sb(f"xg{i}", [SLOT_TILE, SLOT_TILES, REC]) for i in range(2)]
        xgT = [sb(f"xgT{i}", [128, SLOTS]) for i in range(2)]
        hid = [sb(f"hid{i}", [128, FC, SLOTS]) for i in range(2)]
        weight_s = [sb(f"weight_s{i}", [SLOT_TILE, SLOT_TILES]) for i in range(2)]
        obias = sb("obias", [SLOT_TILE, SLOT_TILES, D])
        ow = [sb(f"ow{i}", [SLOT_TILE, SLOT_TILES, D]) for i in range(2)]
        far_s = [sb(f"far_s{i}", [SLOT_TILE, SLOT_TILES]) for i in range(2)]
        dst_i = [sb(f"dst_i{i}", [SLOT_TILE, SLOT_TILES], i32) for i in range(2)]

        chosen = sb("chosen", [128, PAIRS, TOP_K, D])
        zeros = chosen[:].rearrange("p n k d -> p (n k d)")

        bank = [stack.enter_context(nc.psum_tensor(f"bank{i}", [128, 512], f32)) for i in range(8)]
        score_b = [[bank[0], bank[1]], [bank[2], bank[0]]]
        probT_b = bank[4:6]
        post_b, front_b, mix_b = bank[3], bank[6], bank[7]
        av_p = mix_b[:, 0:HP * VW]
        post_p = post_b[:, 0:GT]
        gate_p = post_b[:, GT:GT + GP * E]
        rank_p = mix_b[:, HP * VW:HP * VW + GP * E]

        x0_in, x_in, w_in, bo_in, wl_in, wb_in, mask_in = (
            sem(n) for n in ("x0_in", "x_in", "w_in", "bo_in", "wl_in", "wb_in", "mask_in"))
        ctxk_in, stacks_in, parts_out = (sem(n) for n in ("ctxk_in", "stacks_in", "parts_out"))
        mean_done, meanT_d, meanT_ev, slow_dma, slow_step = (
            sem(n) for n in ("mean_done", "meanT_d", "meanT_ev", "slow_dma", "slow_step"))
        slots_cleared, choices_cleared = sem("slots_cleared"), sem("choices_cleared")
        passed = {n: sem(f"passed_{n}") for n in ("dve", "pool")}
        const_step, const_done, bias_step, bias_done = (
            sem(n) for n in ("const_step", "const_done", "bias_step", "bias_done"))
        x0_clear, x_clear, ctxk_clear, ctxvT_clear, mask_clear, zeros_done, probs_clear, vals_clear = (
            sem(n) for n in ("x0_clear", "x_clear", "ctxk_clear", "ctxvT_clear", "mask_clear", "zeros_done",
                             "probs_clear", "vals_clear"))
        ident_done, vconst = sem("ident_done"), sem("vconst")
        kept_done, flag_step, flag_done, bqs_done = (sem(n) for n in ("kept_done", "flag_step", "flag_done", "bqs_done"))
        stat1_d, mv1_d, ve1_d, rs1_d, nb1_d, xn_d = (
            sem(n) for n in ("stat1_d", "mv1_d", "ve1_d", "rs1_d", "nb1_d", "xn_d"))
        frontT_d, frontT_ev, qk_d, qk_ev = (sem(n) for n in ("frontT_d", "frontT_ev", "qk_d", "qk_ev"))
        hi_d, rest_d, mid_d, lo_d = (sem(n) for n in ("hi_d", "rest_d", "mid_d", "lo_d"))
        vT_ev, v_d, vals_d = (sem(n) for n in ("vT_ev", "v_d", "vals_d"))
        score_d, max_d, sub_d, exp_d = (sem(n) for n in ("score_d", "max_d", "sub_d", "exp_d"))
        probT_d, probT_ev, av_d, rden_d, y_d = (sem(n) for n in ("probT_d", "probT_ev", "av_d", "rden_d", "y_d"))
        yT_d, yT_ev, o_d, xbo_d, x2_d = (sem(n) for n in ("yT_d", "yT_ev", "o_d", "xbo_d", "x2_d"))
        stat2_d, mv2_d, ve2_d, rs2_d, nb2_d, xn2_d = (
            sem(n) for n in ("stat2_d", "mv2_d", "ve2_d", "rs2_d", "nb2_d", "xn2_d"))
        xn2T_d, xn2T_ev, gate_d, lsub_d, lexp_d = (sem(n) for n in ("xn2T_d", "xn2T_ev", "gate_d", "lsub_d", "lexp_d"))
        route, weight_d, taken_d, earlier_d, rank_d, place, rec_free, rec_d, recw_d, slot_d, disp_out = (
            sem(n) for n in ("route", "weight_d", "taken_d", "earlier_d", "rank_d", "place", "rec_free", "rec_d", "recw_d", "slot_d",
                             "disp_out"))
        w1_in = [sem(f"w1_in{i}") for i in range(2)]
        w2_in = [sem(f"w2_in{i}") for i in range(2)]
        xg_in = [sem(f"xg_in{i}") for i in range(2)]
        xgT_d, xgT_ev, up_d, hid_a, hid_v = (sem(n) for n in ("xgT_d", "xgT_ev", "up_d", "hid_a", "hid_v"))
        down_d, wgt_d, far_d, dst_d, obias_d, ow_d = (
            sem(n) for n in ("down_d", "wgt_d", "far_d", "dst_d", "obias_d", "ow_d"))
        comb_out = [sem(f"comb_out{i}") for i in range(2)]
        chosen_in = [sem(f"chosen_in{c}") for c in range(len(CHUNKS))]
        sum_step, out_d, out_out = (sem(n) for n in ("sum_step", "out_d", "out_out"))

        block = stack.enter_context(nc.Block())

        def pipeline(eng, it):
            first, last = 2, GROUPS - 3
            for g in range(-3, first):
                it(g, g)
            with eng.Fori(first, last) as g:
                it(g, first)
            for g in range(last, GROUPS + 2):
                it(g, g)

        def stages(s):
            return (s + 3 < GROUPS, 0 <= s + 2 < GROUPS, 0 <= s + 1 < GROUPS, 0 <= s < GROUPS,
                    0 <= s - 1 < GROUPS, 0 <= s - 2)

        xv = x.rearrange("(n j) q d -> j q n d", j=2)
        ctx_keys = ctx.rearrange("(n j) s d -> j s n d", j=2)
        maskv = mask.rearrange("(n j) q k -> j q n k", j=2)
        slots_v = slots_d.rearrange("(e t p) r -> e p t r", t=SLOT_TILES, p=SLOT_TILE)
        outv = out.rearrange("(n j) q d -> j q n d", j=2)
        choice_v = choice_d.rearrange("(n k p) d -> p n k d", k=TOP_K, p=128)
        w1v = w1
        w2v = w2.rearrange("e (f p) d -> e p f d", p=128)

        @block.sync
        def _(sp):
            def load_keys(t):
                for j in range(2):
                    sp.dma_start(ctxk[PAD * j:PAD * j + S, :, :], ctx_keys[j, 0:S, bass.ds(GP * t, GP), :])\
                        .then_inc(ctxk_in, 16)

            sp.wait_ge(x0_clear, 1)
            for j in range(2):
                sp.dma_start(xs[PAD * j:PAD * j + S, 0:GP, :], xv[j, :, 0:GP, :]).then_inc(x0_in, 16)
            sp.wait_ge(ctxk_clear, 1)
            load_keys(0)
            for to, frm in ((wq_s, wq), (wk_s, wk)):
                sp.dma_start(to[:], frm).then_inc(w_in, 16)
            for to, frm in ((bq_s, bq), (bk_s, bk)):
                sp.dma_start(to[:], frm.rearrange("(p o) -> p o", o=1)).then_inc(w_in, 16)
            sp.wait_ge(mask_clear, 1)
            for j in range(2):
                sp.dma_start(m8[PAD * j:PAD * j + S, :, :], maskv[j, :, :, 0:S]).then_inc(mask_in, 16)
            sp.wait_ge(x_clear, 1)
            for j in range(2):
                sp.dma_start(xs[PAD * j:PAD * j + S, GP:, :], xv[j, :, GP:, :]).then_inc(x_in, 16)
            sp.dma_start(bo_s[:], bo.partition_broadcast(128)).then_inc(bo_in, 16)
            for to, frm in ((wv_s, wv), (wo_s, wo), (gw_s, gate_w)):
                sp.dma_start(to[:], frm).then_inc(wl_in, 16)
            sp.dma_start(bv_s[:], bv.rearrange("(p o) -> p o", o=1)).then_inc(wl_in, 16)
            sp.dma_start(gb_s[:], gate_b.partition_broadcast(128)).then_inc(wl_in, 16)

            def it(g, s):
                norm, front, values, attn, router, dispatch = stages(s)
                if norm and s > -3:
                    wait(sp, frontT_d, g + 3)
                    load_keys(g + 3)
                if values:
                    wait(sp, score_d, 4 * g + 4)
                    sp.wait_ge(parts_out, 16 * STACK_WRITES * (g + 2))
                    for to, which in ((q6, 0), (k6, 1)):
                        sp.dma_start(to[:], stacks_d[g + 1, which].rearrange("s (d h) t -> (s d) h t", h=H))\
                            .then_inc(stacks_in, 16)
                if s == 1:
                    sp.wait_ge(stacks_in, 32 * (s + 2))
                    sp.wait_ge(zeros_done, 1)
                    sp.dma_start(slots_d.rearrange("(p a) r -> p (a r)", p=SLOT_TILE),
                                 zeros[0:SLOT_TILE, 0:E * SLOT_TILES * REC]).then_inc(slots_cleared, 16)
                if s == GROUPS - 3:
                    sp.wait_ge(stacks_in, 32 * (s + 2))
                    sp.dma_start(b1_s[:], b1).then_inc(wb_in, 16)
                    sp.dma_start(b2_s[:], b2.rearrange("e d -> (e d)").partition_broadcast(128)
                                 .rearrange("p (e d) -> p e d", e=E)).then_inc(wb_in, 16)
                    for i in range(2):
                        sp.dma_start(w1_s[i][:], w1v[i]).then_inc(w1_in[i], 16)
                        sp.dma_start(w2_s[i][:], w2v[i]).then_inc(w2_in[i], 16)
                if s == GROUPS - 1:
                    sp.wait_ge(stacks_in, 32 * GROUPS)
                    sp.dma_start(choice_d.rearrange("(p a) r -> p (a r)", p=128), zeros).then_inc(choices_cleared, 16)
                if front:
                    sp.wait_ge(lo_d, g + 3)
                    to = stacks_d[g + 2].rearrange("w s c t -> w c s t")
                    for a in range(2):
                        sp.dma_start(to[0, :, 2 * a:2 * a + 2, :], parts[:, 0, a:a + 1, :].broadcast_to([D, 2, GT]))\
                            .then_inc(parts_out, 16)
                        sp.dma_start(to[1, :, 2 * a:2 * a + 2, :], parts[:, 1, 0:2, :]).then_inc(parts_out, 16)
                    sp.dma_start(to[0, :, 4:6, :], parts[:, 0, 0:3:2, :]).then_inc(parts_out, 16)
                    for slot, part in ((4, 2), (5, 0)):
                        sp.dma_start(to[1, :, slot, :], parts[:, 1, part, :]).then_inc(parts_out, 16)
            pipeline(sp, it)

            def load_slots(e, i, first):
                if not first:
                    sp.wait_ge(xgT_d, e - 1)
                    sp.wait_ge(dst_d, e - 1)
                sp.dma_start(xg[i][:], slots_v[e]).then_inc(xg_in[i], 16)

            def load_weights(e, i):
                sp.wait_ge(up_d, FC * (e - 1))
                sp.dma_start(w1_s[i][:], w1v[e]).then_inc(w1_in[i], 16)
                sp.wait_ge(down_d, e - 1)
                sp.dma_start(w2_s[i][:], w2v[e]).then_inc(w2_in[i], 16)

            sp.wait_ge(disp_out, 16 * TOP_K * PAIRS)
            load_slots(0, 0, True)
            load_slots(1, 1, True)
            with sp.Fori(1, E // 2) as two:
                for i in range(2):
                    load_slots(2 * two + i, i, False)
                    load_weights(2 * two + i, i)
            for i in range(2):
                sp.wait_ge(comb_out[i], 16 * SLOT_TILES * E // 2)
            for c, (n, size) in enumerate(CHUNKS):
                sp.dma_start(chosen[:, n:n + size], choice_v[:, n:n + size]).then_inc(chosen_in[c], 16)
            for c, (n, size) in enumerate(CHUNKS):
                sp.wait_ge(out_d, c + 1)
                for j in range(2):
                    sp.dma_start(outv[j, :, n:n + size, :], x2[PAD * j:PAD * j + S, n:n + size, :])\
                        .then_inc(out_out, 16)
            sp.wait_ge(out_out, 32 * len(CHUNKS))
            sp.wait_ge(parts_out, 16 * STACK_WRITES * GROUPS)
            sp.wait_ge(slots_cleared, 16)
            sp.wait_ge(choices_cleared, 16)

        @block.gpsimd
        def _(pool):
            gp = nc.gpsimd
            gp.memset(causal[:], 1.0).then_inc(const_step, 1)
            gp.memset(ident[:], 0.0).then_inc(const_step, 1)
            gp.memset(before[:], 1.0).then_inc(const_step, 1)
            pool.wait_ge(const_step, 3)
            gp.affine_select(out=ident[:], in_=ident[:], compare_op=ALU.not_equal, fill=1.0, base=0,
                             pattern=[[-1, 128]], channel_multiplier=1).then_inc(ident_done, 1)
            gp.affine_select(out=before[:], in_=before[:], compare_op=ALU.is_ge, fill=0.0, base=0,
                             pattern=[[1, 128]], channel_multiplier=-1).then_inc(const_step, 1)
            gp.memset(minus_half[:], -0.5).then_inc(const_step, 1)
            gp.iota(slot_base_i[:], [[SLOTS, E]], base=-1, channel_multiplier=0).then_inc(const_step, 1)
            gp.iota(expert_i[:], [[1, E]], base=0, channel_multiplier=0).then_inc(const_step, 1)
            gp.iota(dest_i[:], [[128, TOP_K], [TOP_K * 128, PAIRS]], base=1, channel_multiplier=1).then_inc(const_step, 1)
            gp.memset(mean[:], 0.0).then_inc(const_step, 1)
            for j in range(2):
                pool.wait_ge(const_step, 9 + j)
                gp.affine_select(out=causal[PAD * j:PAD * (j + 1)], in_=causal[PAD * j:PAD * (j + 1)],
                                 compare_op=ALU.is_ge, fill=0.0, base=0, pattern=[[-1, S]],
                                 channel_multiplier=1).then_inc(const_step, 1)
            pool.wait_ge(const_step, 11)

            def means():
                pool.wait_ge(flag_done, 1)
                flag = pool.value_load(all_gone[0:1, 0:1], min_val=0, max_val=1)
                with pool.If(flag > 0):
                    gp.memset(key_sum[:], 0.0).then_inc(slow_step, 1)
                    quarters = ctx.rearrange("b (w c k) d -> (b w) c k d", w=KQ, k=KCH)
                    with pool.Fori(0, N_KCH) as c:
                        pool.wait_ge(slow_step, c * KCH + 1)
                        pool.dma_start(keys_c[:], quarters[:, c]).then_inc(slow_dma, 16)
                        pool.wait_ge(slow_dma, c * 16 + 16)
                        hold(pool, passed["pool"])
                        with pool.Fori(0, KCH) as k:
                            pool.wait_ge(slow_step, c * KCH + k + 1)
                            gp.tensor_tensor(key_sum[:], key_sum[:], keys_c[:, k, :], add).then_inc(slow_step, 1)
                    pool.wait_ge(slow_step, N_KCH * KCH + 1)
                    pool.dma_start(sums_d, key_sum[:]).then_inc(slow_dma, 16)
                    pool.wait_ge(slow_dma, 16 * N_KCH + 16)
                    pool.dma_start(quarter[:], sums_d.rearrange("(b w) d -> b w d", w=KQ)).then_inc(slow_dma, 16)
                    pool.wait_ge(slow_dma, 16 * N_KCH + 32)
                    for w in range(KQ):
                        gp.tensor_tensor(mean[:], mean[:], quarter[:, w, :], add).then_inc(slow_step, 1)
                        pool.wait_ge(slow_step, N_KCH * KCH + 2 + w)
                    gp.tensor_scalar(mean[:], mean[:], 1.0 / S2, None, mult).then_inc(slow_step, 1)
                    pool.wait_ge(slow_step, N_KCH * KCH + 2 + KQ)
                pool.sem_inc(mean_done, 1)

            pool.sem_inc(rec_free, 1)

            def it(g, s):
                norm, front, values, attn, router, dispatch = stages(s)
                if s == -2:
                    gp.memset(chosen[:], 0.0).then_inc(zeros_done, 1)
                    for p in range(GP):
                        gp.memset(probs[p][:], 0.0).then_inc(probs_clear, 1)
                def scatter(p):
                    for k in range(TOP_K):
                        gp.indirect_dma_start(
                            out=slots_d, out_offset=bass.IndirectOffsetOnAxis(ap=slot_i[:, k, p:p + 1], axis=0),
                            in_=rec[:, k, p, :], in_offset=None, bounds_check=E * SLOTS - 1,
                            oob_is_err=False).then_inc(disp_out, 16)

                if router:
                    pool.wait_ge(ve2_d, g)
                    gp.tensor_tensor(rs2[:], ve2[:], minus_half[:], ALU.pow).then_inc(rs2_d, 1)
                if dispatch:
                    pool.wait_ge(rec_d, 2 * (g - 1))
                    pool.wait_ge(recw_d, g - 1)
                    pool.wait_ge(slot_d, g - 1)
                    hold(pool, passed["pool"])
                    if s == 2:
                        pool.wait_ge(slots_cleared, 16)
                    scatter(0)
                if norm:
                    pool.wait_ge(ve1_d, g + 4)
                    wait(pool, xn_d, GP * (g + 3))
                    gp.tensor_tensor(rs1[:], ve1[:], minus_half[:], ALU.pow).then_inc(rs1_d, 1)
                if front:
                    pool.wait_ge(hi_d, g + 3)
                    gp.tensor_tensor(rest[:], qk[:], parts[:, :, 0, :], sub).then_inc(rest_d, 1)
                if front:
                    pool.wait_ge(mid_d, g + 3)
                    pool.wait_ge(rest_d, g + 3)
                    gp.tensor_tensor(parts[:, :, 2, :], rest[:], parts[:, :, 1, :], sub).then_inc(lo_d, 1)
                if s == -2:
                    means()
                if dispatch:
                    scatter(1)
                if front:
                    if s == -2:
                        pool.wait_ge(x_in, 32)
                        pool.wait_ge(bo_in, 16)
                    t = g + 2
                    gp.tensor_tensor(x2[:, bass.ds(GP * t, GP), :], xs[:, bass.ds(GP * t, GP), :],
                                     bo_s[:].unsqueeze(1).broadcast_to([128, GP, D]), add).then_inc(xbo_d, 1)
                if dispatch:
                    pool.wait_ge(disp_out, 64 * (g - 1))
                    pool.sem_inc(rec_free, 1)

            pipeline(pool, it)

            def send(e, i):
                if isinstance(e, int) and e == 0:
                    pool.wait_ge(choices_cleared, 16)
                pool.wait_ge(ow_d, e + 1)
                hold(pool, passed["pool"])
                for t in range(SLOT_TILES):
                    gp.indirect_dma_start(
                        out=choice_d, out_offset=bass.IndirectOffsetOnAxis(ap=dst_i[i][:, t:t + 1], axis=0),
                        in_=ow[i][:, t, :], in_offset=None, bounds_check=N_DST - 1,
                        oob_is_err=False).then_inc(comb_out[i], 16)

            send(0, 0)
            send(1, 1)
            with pool.Fori(1, E // 2) as two:
                send(2 * two, 0)
                send(2 * two + 1, 1)

        @block.scalar
        def _(act):
            sc = nc.scalar

            def it(g, s):
                norm, front, values, attn, router, dispatch = stages(s)

                def exponentials(p, i):
                    act.wait_ge(sub_d, 4 * g + 2 * p + i + 1)
                    heads = probs[p][:, 8 * i:8 * i + 8, 0:KEYS]
                    sc.activation(heads, heads, ACT.Exp).then_inc(exp_d, 1)

                def evacuate(p):
                    for i in range(2):
                        act.wait_ge(probT_d, 4 * g + 2 * p + i + 1)
                        sc.activation(probsT[p][:, 4 * i:4 * i + 4, :].rearrange("a h q -> a (h q)"), probT_b[i][:],
                                      ACT.Copy).then_inc(probT_ev, 1)

                def normalise(to, tiles, t, scale, shift, done):
                    for p in range(GP):
                        sc.activation(to[:, p, :], tiles[:, GP * t + p, :], ACT.Identity, bias=shift[:, p:p + 1],
                                      scale=scale[:, p:p + 1]).then_inc(done, 1)

                if router:
                    if s == 1:
                        act.wait_ge(wl_in, 80)
                    act.wait_ge(yT_d, g)
                    sc.activation(yT[:], post_p, ACT.Identity, bias=bv_s[:]).then_inc(yT_ev, 1)
                if values:
                    if s == -1:
                        act.wait_ge(meanT_ev, 1)
                        act.wait_ge(ctxvT_clear, 1)
                    act.wait_ge(frontT_ev, g + 2)
                    wait(act, v_d, g + 1)
                    twice = [128, 2 * GP, 2, S]
                    sc.activation(ctxvT[:, :, :, 0:S], frontT[:, 1, :].rearrange("p (b k) -> p b k", k=PAD)[:, :, 0:S]
                                  .unsqueeze(2).broadcast_to(twice), ACT.Copy).then_inc(vT_ev, 1)
                    sc.activation(ctxvT[:, :, :, S], meanT[:, bass.ds(2 * GP * (g + 1), 2 * GP)].unsqueeze(2)
                                  .broadcast_to([128, 2 * GP, 2]), ACT.Copy).then_inc(vT_ev, 1)
                if front:
                    wait(act, vT_ev, 2 * (g + 2))
                    act.wait_ge(frontT_d, g + 3)
                    sc.activation(frontT[:].rearrange("p a t -> p (a t)"), front_b[:], ACT.Copy).then_inc(frontT_ev, 1)
                if attn:
                    exponentials(0, 0)
                    exponentials(0, 1)
                if attn:
                    evacuate(0)
                if dispatch:
                    act.wait_ge(rec_free, g - 1)
                    act.wait_ge(xn2_d, GP * (g - 1))
                    sc.activation(rec[:, :, :, 0:D], xn2[:].unsqueeze(1).broadcast_to([128, TOP_K, GP, D]), ACT.Copy)\
                        .then_inc(rec_d, 1)
                    sc.activation(rec[:, :, :, D + 1], dest[:, :, bass.ds(GP * (g - 2), GP)], ACT.Copy)\
                        .then_inc(rec_d, 1)
                if attn:
                    exponentials(1, 0)
                if router:
                    act.wait_ge(nb2_d, g)
                    wait(act, xn2T_d, g - 1)
                    if dispatch:
                        act.wait_ge(rec_d, 2 * (g - 1) - 1)
                    normalise(xn2, x2, g - 1, rs2, nb2, xn2_d)
                if attn:
                    exponentials(1, 1)
                if router:
                    act.wait_ge(xn2T_d, g)
                    sc.activation(xn2T[:], post_p, ACT.Copy).then_inc(xn2T_ev, 1)
                if front:
                    if s == -2:
                        act.wait_ge(bqs_done, 1)
                        act.wait_ge(w_in, 64)
                    act.wait_ge(qk_d, g + 3)
                    wait(act, lo_d, g + 2)
                    sc.activation(qk[:, 0, :], front_b[:, 0:GT], ACT.Identity, bias=bqs[:],
                                  scale=float(1.0 / np.sqrt(np.float32(HD)))).then_inc(qk_ev, 1)
                    sc.activation(qk[:, 1, :], front_b[:, GT:2 * GT], ACT.Identity, bias=bk_s[:])\
                        .then_inc(qk_ev, 1)
                if attn:
                    evacuate(1)
                if front:
                    act.wait_ge(qk_ev, 2 * (g + 3))
                    wait(act, parts_out, 16 * STACK_WRITES * (g + 2))
                    sc.activation(parts[:, :, 0, :], qk[:], ACT.Copy).then_inc(hi_d, 1)
                if router:
                    act.wait_ge(lsub_d, g)
                    sc.activation(prob[:], logit[:], ACT.Exp).then_inc(lexp_d, 1)
                if norm:
                    act.wait_ge(nb1_d, g + 4)
                    wait(act, frontT_d, g + 3)
                    normalise(xn, xs, g + 3, rs1, nb1, xn_d)
                if front:
                    act.wait_ge(rest_d, g + 3)
                    sc.activation(parts[:, :, 1, :], rest[:], ACT.Copy).then_inc(mid_d, 1)
                if values:
                    if s == -1:
                        act.wait_ge(vals_clear, 2)
                    act.wait_ge(v_d, g + 2)
                    wait(act, av_d, 2 * (g + 1))
                    for j in range(2):
                        half = slice(PAD * j, PAD * (j + 1))
                        sc.activation(vals[half, :, :, (HD + 1) * j:(HD + 1) * j + HD],
                                      front_b[half, :].rearrange("k (b h two d) -> k b h two d", b=2 * GP, two=2, d=HD)
                                      [:, :, :, j, :], ACT.Copy).then_inc(vals_d, 1)

            pipeline(act, it)
            act.wait_ge(wb_in, 32)

            def expert(e, i):
                act.wait_ge(xgT_d, e + 1)
                sc.activation(xgT[i][:], probT_b[i][:, 0:SLOTS], ACT.Copy).then_inc(xgT_ev, 1)
                for f in (0, 2):
                    act.wait_ge(up_d, FC * e + f + 1)
                    sc.activation(hid[i][:, f, :], bank[f][:, 0:SLOTS], ACT.Relu, bias=b1_s[:, e, f:f + 1])\
                        .then_inc(hid_a, 1)

            with act.Fori(0, E // 2) as two:
                expert(2 * two, 0)
                expert(2 * two + 1, 1)

        @block.vector
        def _(dve):
            ve = nc.vector

            def constants():
                dve.wait_ge(ident_done, 1)
                ve.tensor_copy(ident_b[:], ident[:]).then_inc(vconst, 1)
                ve.reduce_sum(row_ok[:], ident[:].rearrange("p (j q) -> p j q", j=2)[:, :, 0:S], mybir.AxisListType.XY)\
                    .then_inc(vconst, 1)
                ve.memset(valid[:], 1.0).then_inc(vconst, 1)
                dve.wait_ge(const_step, 9)
                dve.wait_ge(vconst, 3)
                ve.tensor_scalar(before[:], before[:], row_ok[:], None, mult).then_inc(vconst, 1)
                ve.tensor_scalar(valid[:], valid[:], row_ok[:], None, mult).then_inc(vconst, 1)
                ve.tensor_scalar(row_far[:], row_ok[:], -FAR, FAR, mult, add).then_inc(vconst, 1)
                ve.tensor_copy(expert_no[:], expert_i[:]).then_inc(vconst, 1)
                ve.tensor_copy(dest[:], dest_i[:]).then_inc(vconst, 1)
                dve.wait_ge(vconst, 8)
                ve.tensor_scalar(slot_base[:], slot_base_i[:], row_far[:], None, add).then_inc(const_done, 1)

            ve.memset(xs[:, 0:GP, :], 0.0).then_inc(x0_clear, 1)
            ve.memset(ctxk[:], 0.0).then_inc(ctxk_clear, 1)
            ve.memset(m8[:].rearrange("p a b -> p (a b)").bitcast(i32), 0).then_inc(mask_clear, 1)
            ve.memset(xs[:, GP:, :], 0.0).then_inc(x_clear, 1)
            ve.memset(ctxvT[:], 0.0).then_inc(ctxvT_clear, 1)

            def mask_to_bias():
                dve.wait_ge(mask_in, 32)
                dve.wait_ge(const_step, 11)
                ve.tensor_tensor(mc[:], m8[:], causal[:].unsqueeze(1).broadcast_to([128, PAIRS, S]), mult)\
                    .then_inc(bias_step, 1)
                ve.memset(bias[:], GONE).then_inc(bias_step, 1)
                dve.wait_ge(bias_step, 2)
                ve.reduce_max(some[:], mc[:], X).then_inc(bias_step, 1)
                dve.wait_ge(bias_step, 3)
                ve.tensor_scalar(bias[:, :, 0:S], mc[:], -1.0, -GONE, add, mult)
                ve.tensor_scalar(bias[:, :, S], some[:], GONE, None, mult).then_inc(bias_done, 1)
                dve.wait_ge(kept_done, 1)
                ve.reduce_sum(rows_kept[:], mix_b[0:1, 0:PAIRS], X).then_inc(flag_step, 1)
                dve.wait_ge(flag_step, 1)
                ve.tensor_scalar(all_gone[:], rows_kept[:], B * S - 0.5, None, ALU.is_lt).then_inc(flag_done, 1)
            dve.wait_ge(x0_in, 32)

            def stats(t, tiles, stat, stat_d):
                for p in range(GP):
                    ve.bn_stats(stat[:, p, :], tiles[:, GP * t + p, :]).then_inc(stat_d, 1)

            def mean_variance(t, stat, mv, stat_d, mv_d):
                wait(dve, stat_d, GP * (t + 1))
                hold(dve, passed["dve"])
                for p in range(GP):
                    ve.bn_aggr(mv[:, p, :], stat[:, p, :]).then_inc(mv_d, 1)

            def add_eps(t, mv, vee, mv_d, ve_d):
                wait(dve, mv_d, GP * (t + 1))
                ve.tensor_scalar(vee[:], mv[:, :, 1], 1e-5, None, add).then_inc(ve_d, 1)

            def shift(t, mv, rs, nb, rs_d, nb_d):
                wait(dve, rs_d, t + 1)
                ve.scalar_tensor_tensor(nb[:], mv[:, :, 0], -1.0, rs[:], mult, mult).then_inc(nb_d, 1)

            def scale_bias():
                dve.wait_ge(w_in, 64)
                ve.tensor_scalar(bqs[:], bq_s[:], float(1.0 / np.sqrt(np.float32(HD))), None, mult)\
                    .then_inc(bqs_done, 1)

            def clear_buffers():
                ve.memset(earlier[:], 0.0).then_inc(earlier_d, 1)
                ve.memset(vals[:], 0.0).then_inc(vals_clear, 1)
                dve.wait_ge(vals_clear, 1)
                ve.memset(vals[0:PAD, :, :, HD], 1.0)
                ve.memset(vals[PAD:128, :, :, VW - 1], 1.0).then_inc(vals_clear, 1)

            def it(g, s):
                norm, front, values, attn, router, dispatch = stages(s)

                def maxima(p, i):
                    dve.wait_ge(score_d, 4 * g + 2 * p + i + 1)
                    ve.reduce_max(row_max[:, p, 8 * i:8 * i + 8],
                                  score_b[p][i][:].rearrange("q (h k) -> q h k", k=PAD)[:, :, 0:KEYS], X)\
                        .then_inc(max_d, 1)

                def less_maxima(p, i):
                    if i == 0:
                        wait(dve, probT_d, 4 * (g - 1) + 2 * p + 2)
                    dve.wait_ge(max_d, 4 * g + 2 * p + i + 1)
                    ve.tensor_tensor(probs[p][:, 8 * i:8 * i + 8, 0:KEYS],
                                     score_b[p][i][:].rearrange("q (h k) -> q h k", k=PAD)[:, :, 0:KEYS],
                                     row_max[:, p, 8 * i:8 * i + 8].unsqueeze(2).broadcast_to([128, 8, KEYS]), sub)\
                        .then_inc(sub_d, 1)

                def divide(p, t):
                    dve.wait_ge(av_d, 2 * t + p + 1)
                    heads = av_p.rearrange("q (h d) -> q h d", d=HD + 1)
                    ve.reciprocal(rden[:, p, :], heads[:, :, HD]).then_inc(rden_d, 1)
                    dve.wait_ge(rden_d, 2 * t + p + 1)
                    ve.tensor_tensor(y[:, p, :].rearrange("q (h d) -> q h d", d=HD), heads[:, :, 0:HD],
                                     rden[:, p, :].unsqueeze(2).broadcast_to([128, H, HD]), mult).then_inc(y_d, 1)

                def per_tile(ap):
                    return ap.unsqueeze(2).broadcast_to([128, GP, E])

                def ranks():
                    t = g - 2
                    dve.wait_ge(rank_d, t + 1)
                    rank = rank_p.rearrange("q (p e) -> q p e", e=E)
                    ve.tensor_scalar(over[:], rank, CAP + 0.5, FAR, ALU.is_gt, mult).then_inc(place, 1)
                    ve.tensor_tensor(slot_e[:], rank, slot_base[:].unsqueeze(1).broadcast_to([128, GP, E]), add)\
                        .then_inc(place, 1)
                    ve.tensor_tensor(earlier[:, 0, :], earlier[:, 1, :], taken[:, 1, :], add).then_inc(earlier_d, 1)

                def slots_of_experts():
                    dve.wait_ge(place, 4 * (g - 2) + 2)
                    ve.tensor_tensor(slot_e[:], slot_e[:], over[:], add).then_inc(place, 1)

                def slots_of_choices():
                    dve.wait_ge(place, 4 * (g - 2) + 3)
                    ve.tensor_tensor(slot_k[:], onehot[:], slot_e[:].unsqueeze(1)
                                     .broadcast_to([128, TOP_K, GP, E]), mult).then_inc(place, 1)

                def slots():
                    dve.wait_ge(place, 4 * (g - 1))
                    dve.wait_ge(rec_free, g - 1)
                    dve.wait_ge(weight_d, g - 1)
                    ve.tensor_copy(rec[:, :, :, D], weight[:]).then_inc(recw_d, 1)
                    with nc.allow_low_precision(reason="slots are whole numbers, summed in float32"):
                        ve.reduce_sum(slot_i[:], slot_k[:], X).then_inc(slot_d, 1)

                def residual():
                    dve.wait_ge(o_d, g)
                    dve.wait_ge(xbo_d, g)
                    tiles = x2[:, bass.ds(GP * (g - 1), GP), :].rearrange("q p d -> q (p d)")
                    ve.tensor_tensor(tiles, tiles, post_p, add).then_inc(x2_d, 1)

                def step(ins):
                    ins.then_inc(route, 1)

                def after(t, steps):
                    dve.wait_ge(route, ROUTE * t + steps)

                def logits(t):
                    dve.wait_ge(gate_d, t + 1)
                    step(ve.tensor_tensor(logit[:], gate_p.rearrange("q (p e) -> q p e", e=E),
                                          gb_s[:].unsqueeze(1).broadcast_to([128, GP, E]), add))
                    after(t, 1)
                    step(ve.reduce_max(lmax[:], logit[:], X))
                    after(t, 2)
                    ve.tensor_tensor(logit[:], logit[:], per_tile(lmax[:]), sub).then_inc(lsub_d, 1)

                def experts_probs(t):
                    dve.wait_ge(lexp_d, t + 1)
                    step(ve.reduce_sum(esum[:], prob[:], X))
                    after(t, 3)
                    step(ve.reciprocal(esum[:], esum[:]))
                    after(t, 4)
                    step(ve.tensor_tensor(prob[:], prob[:], per_tile(esum[:]), mult))
                    after(t, 5)
                    hold(dve, passed["dve"])
                    for p in range(GP):
                        step(ve.max(top[:, p, :], prob[:, p, :]))

                def two_greatest(t):
                    after(t, 5 + GP)
                    hold(dve, passed["dve"])
                    for p in range(GP):
                        step(ve.max_index(top_i[:, p, :], top[:, p, :], prob[:, p, :]))
                    step(ve.tensor_tensor(topsum[:], top[:, :, 0], top[:, :, 1], add))

                def choices(t):
                    after(t, 6 + 2 * GP)
                    step(ve.tensor_tensor(onehot[:], expert_no[:].unsqueeze(1).unsqueeze(1)
                                          .broadcast_to([128, TOP_K, GP, E]),
                                          top_i[:, :, 0:TOP_K].rearrange("q p k -> q k p").unsqueeze(3)
                                          .broadcast_to([128, TOP_K, GP, E]), ALU.is_equal))
                    step(ve.reciprocal(topsum[:], topsum[:]))

                def weights(t):
                    after(t, 8 + 2 * GP)
                    ve.tensor_tensor(taken[:], onehot[:, 0], onehot[:, 1], add).then_inc(taken_d, 1)
                    ve.tensor_tensor(weight[:], top[:, :, 0:TOP_K].rearrange("q p k -> q k p"),
                                     topsum[:].unsqueeze(1).broadcast_to([128, TOP_K, GP]), mult).then_inc(weight_d, 1)

                def add_earlier(t):
                    dve.wait_ge(taken_d, t + 1)
                    dve.wait_ge(earlier_d, 2 * t + 1)
                    ve.tensor_tensor(earlier[:, 1, :], earlier[:, 0, :], taken[:, 0, :], add).then_inc(earlier_d, 1)

                if s == -2:
                    scale_bias()
                    clear_buffers()
                    dve.wait_ge(x_in, 32)
                if attn:
                    maxima(0, 0)
                if dispatch:
                    two_greatest(g - 2)
                if attn:
                    less_maxima(0, 0)
                if dispatch:
                    choices(g - 2)
                if attn:
                    maxima(0, 1)
                if dispatch:
                    weights(g - 2)
                if attn:
                    less_maxima(0, 1)
                if dispatch:
                    add_earlier(g - 2)
                if router:
                    residual()
                if attn:
                    maxima(1, 0)
                if router:
                    dve.wait_ge(x2_d, g)
                    hold(dve, passed["dve"])
                    stats(g - 1, x2, stat2, stat2_d)
                if dispatch:
                    ranks()
                if router:
                    mean_variance(g - 1, stat2, mv2, stat2_d, mv2_d)
                if dispatch:
                    slots_of_experts()
                if router:
                    add_eps(g - 1, mv2, ve2, mv2_d, ve2_d)
                if attn:
                    less_maxima(1, 0)
                    maxima(1, 1)
                if router:
                    shift(g - 1, mv2, rs2, nb2, rs2_d, nb2_d)
                if dispatch:
                    slots_of_choices()
                if attn:
                    less_maxima(1, 1)
                if dispatch:
                    slots()
                if norm:
                    stats(g + 3, xs, stat1, stat1_d)
                if attn:
                    divide(0, g)
                if norm:
                    mean_variance(g + 3, stat1, mv1, stat1_d, mv1_d)
                    add_eps(g + 3, mv1, ve1, mv1_d, ve1_d)
                if norm and not router:
                    shift(g + 3, mv1, rs1, nb1, rs1_d, nb1_d)
                if s == -2:
                    constants()
                    mask_to_bias()
                    dve.wait_ge(meanT_d, 1)
                    ve.tensor_copy(meanT[:], mix_b[:, 0:B]).then_inc(meanT_ev, 1)
                if router:
                    logits(g - 1)
                if norm and router:
                    shift(g + 3, mv1, rs1, nb1, rs1_d, nb1_d)
                if router:
                    experts_probs(g - 1)
                if attn:
                    divide(1, g)

            ROUTE = 12
            pipeline(dve, it)

            def expert(e, i, first=False):
                for f in (1, 3):
                    dve.wait_ge(up_d, FC * e + f + 1)
                    ve.tensor_scalar(hid[i][:, f, :], bank[f][:, 0:SLOTS], b1_s[:, e, f:f + 1], 0.0, add, ALU.max)\
                        .then_inc(hid_v, 1)
                dve.wait_ge(xg_in[i], 8 * (e - i) + 16)
                if not first:
                    dve.wait_ge(comb_out[i], 8 * SLOT_TILES * (e - i))
                ve.tensor_copy(weight_s[i][:], xg[i][:, :, D]).then_inc(wgt_d, 1)
                ve.tensor_scalar(far_s[i][:], xg[i][:, :, D + 1], 0.5, FAR, ALU.is_lt, mult).then_inc(far_d, 1)
                dve.wait_ge(far_d, e + 1)
                ve.scalar_tensor_tensor(dst_i[i][:], xg[i][:, :, D + 1], -1.0, far_s[i][:], add, add).then_inc(dst_d, 1)
                dve.wait_ge(down_d, e + 1)
                if not first:
                    dve.wait_ge(ow_d, e - 1)
                ve.tensor_tensor(obias[:], bank[6 + i][0:SLOT_TILE, 0:SLOT_TILES * D].rearrange("s (t d) -> s t d", d=D),
                                 b2_s[0:SLOT_TILE, e, :].unsqueeze(1).broadcast_to([SLOT_TILE, SLOT_TILES, D]), add)\
                    .then_inc(obias_d, 1)
                dve.wait_ge(obias_d, e + 1)
                dve.wait_ge(wgt_d, e + 1)
                ve.tensor_tensor(ow[i][:], obias[:],
                                 weight_s[i][:].unsqueeze(2).broadcast_to([SLOT_TILE, SLOT_TILES, D]), mult)\
                    .then_inc(ow_d, 1)

            dve.wait_ge(wb_in, 32)
            expert(0, 0, first=True)
            expert(1, 1, first=True)
            with dve.Fori(1, E // 2) as two:
                expert(2 * two, 0)
                expert(2 * two + 1, 1)
            dve.wait_ge(dst_d, E)
            for c, (n, size) in enumerate(CHUNKS):
                dve.wait_ge(chosen_in[c], 16)
                tiles = x2[:, n:n + size, :]
                ve.tensor_tensor(tiles, tiles, chosen[:, n:n + size, 0, :], add).then_inc(sum_step, 1)
                dve.wait_ge(sum_step, c + 1)
                ve.tensor_tensor(tiles, tiles, chosen[:, n:n + size, 1, :], add).then_inc(out_d, 1)

        @block.tensor
        def _(pe):
            mm, tr = nc.tensor.matmul, nc.tensor.transpose
            pe.wait_ge(ident_done, 1)

            def it(g, s):
                norm, front, values, attn, router, dispatch = stages(s)

                def scores(p, i):
                    wait(pe, sub_d, 4 * g + ((0, -2), (-1, 1))[p][i])
                    rows = bias[:, GP * g + p, :].unsqueeze(1).broadcast_to([128, 8, PAD])
                    mm(score_b[p][i][:], ident_b[:], rows, start=True, stop=False, skip_group_check=True)
                    for h in range(8):
                        for j in range(2):
                            cols = slice(128 * p + PAD * j, 128 * p + PAD * (j + 1))
                            last = mm(score_b[p][i][PAD * j:PAD * (j + 1), PAD * h:PAD * (h + 1)],
                                      q6[:, 8 * i + h, cols], k6[:, 8 * i + h, cols], start=False, stop=True,
                                      skip_group_check=True)
                    last.then_inc(score_d, 1)

                def transpose_probs(p, i):
                    pe.wait_ge(exp_d, 4 * g + 2 * p + i + 1)
                    wait(pe, probT_ev, 4 * g + 2 * p + i - 1)
                    for h in range(4):
                        hp = 4 * i + h
                        last = tr(probT_b[i][:, 128 * h:128 * (h + 1)],
                                  probs[p][:, 2 * hp:2 * hp + 2, :].rearrange("q h k -> q (h k)"), ident[:])
                    last.then_inc(probT_d, 1)

                def mix_values(p):
                    pe.wait_ge(probT_ev, 4 * g + 2 * p + 2)
                    pe.wait_ge(vals_d, 2 * (g + 1))
                    wait(pe, y_d, 2 * g + p)
                    if dispatch:
                        pe.wait_ge(place, 4 * (g - 2) + 2)
                    for j in range(2):
                        for hp in range(HP):
                            last = mm(av_p[PAD * j:PAD * (j + 1), VW * hp:VW * (hp + 1)],
                                      probsT[p][:, hp, PAD * j:PAD * (j + 1)], vals[:, GP * p + j, hp, :],
                                      start=True, stop=True, skip_group_check=True)
                    last.then_inc(av_d, 1)

                if s == -2:
                    pe.wait_ge(w_in, 64)
                def transpose_to_post(tile):
                    for p in range(GP):
                        last = tr(post_p[:, 128 * p:128 * (p + 1)], tile[:, p, :], ident[:])
                    return last

                if attn:
                    if s == 0:
                        pe.wait_ge(bias_done, 1)
                        pe.wait_ge(probs_clear, GP)
                    pe.wait_ge(stacks_in, 32 * (g + 1))
                    scores(0, 0)
                if attn:
                    scores(0, 1)
                if router:
                    pe.wait_ge(y_d, 2 * g)
                    transpose_to_post(y).then_inc(yT_d, 1)
                if attn:
                    scores(1, 0)
                if router:
                    if s == 1:
                        pe.wait_ge(wl_in, 80)
                    pe.wait_ge(yT_ev, g)
                    for p in range(GP):
                        last = mm(post_p[:, 128 * p:128 * (p + 1)], yT[:, 128 * p:128 * (p + 1)], wo_s[:],
                                  start=True, stop=True)
                    last.then_inc(o_d, 1)
                if front:
                    pe.wait_ge(xn_d, GP * (g + 3))
                    pe.wait_ge(ctxk_in, 32 * (g + 3))
                    wait(pe, vals_d, 2 * (g + 1))
                    for p in range(GP):
                        tr(front_b[:, 128 * p:128 * (p + 1)], xn[:, p, :], ident[:])
                        last = tr(front_b[:, GT + 128 * p:GT + 128 * (p + 1)], ctxk[:, p, :], ident[:])
                    last.then_inc(frontT_d, 1)
                if attn:
                    scores(1, 1)
                if dispatch:
                    pe.wait_ge(earlier_d, 2 * (g - 1))
                    pe.wait_ge(y_d, 2 * g if attn else 2 * GROUPS)
                    mm(rank_p, before[:], taken[:].rearrange("q p e -> q (p e)"), start=True, stop=False)
                    mm(rank_p, valid[:], earlier[:].rearrange("q p e -> q (p e)"), start=False, stop=True)\
                        .then_inc(rank_d, 1)
                if attn:
                    transpose_probs(0, 0)
                if attn:
                    transpose_probs(0, 1)
                if front:
                    pe.wait_ge(frontT_ev, g + 3)
                    mm(front_b[:, 0:GT], wq_s[:], frontT[:, 0, :], start=True, stop=True)
                    mm(front_b[:, GT:2 * GT], wk_s[:], frontT[:, 1, :], start=True, stop=True).then_inc(qk_d, 1)
                if s == -2:
                    pe.wait_ge(const_done, 1)
                    pe.wait_ge(bias_step, 3)
                    mm(mix_b[0:1, 0:PAIRS], valid[:, 0:1], some[:], start=True, stop=True).then_inc(kept_done, 1)
                    pe.wait_ge(mean_done, 1)
                    pe.wait_ge(flag_step, 1)
                    tr(mix_b[:, 0:B], mean[:], ident[0:B, 0:B]).then_inc(meanT_d, 1)
                if attn:
                    mix_values(0)
                if attn:
                    transpose_probs(1, 0)
                if router:
                    pe.wait_ge(xn2_d, GP * g)
                    transpose_to_post(xn2).then_inc(xn2T_d, 1)
                if attn:
                    transpose_probs(1, 1)
                if router:
                    pe.wait_ge(xn2T_ev, g)
                    for p in range(GP):
                        last = mm(gate_p[:, E * p:E * (p + 1)], xn2T[:, 128 * p:128 * (p + 1)], gw_s[:],
                                  start=True, stop=True)
                    last.then_inc(gate_d, 1)
                if values:
                    if s == -1:
                        pe.wait_ge(wl_in, 80)
                    if front:
                        pe.wait_ge(qk_ev, 2 * (g + 3))
                    else:
                        pe.wait_ge(vals_d, 2 * (g + 1))
                    pe.wait_ge(vT_ev, 2 * (g + 2))
                    for b in range(2 * GP):
                        last = mm(front_b[:, D * b:D * (b + 1)], ctxvT[:, b, :, :].rearrange("c n k -> c (n k)"),
                                  wv_s[:], start=True, stop=True)
                    last.then_inc(v_d, 1)
                if attn:
                    mix_values(1)

            pipeline(pe, it)

            def transpose_slots(e, i):
                pe.wait_ge(xg_in[i], 8 * (e - i) + 16)
                wait(pe, xgT_ev, e - 1)
                for t in range(SLOT_TILES):
                    last = tr(probT_b[i][:, SLOT_TILE * t:SLOT_TILE * (t + 1)], xg[i][:, t, 0:D],
                              ident[0:SLOT_TILE, 0:SLOT_TILE])
                last.then_inc(xgT_d, 1)

            def expert(e, i, more):
                pe.wait_ge(w1_in[i], 8 * (e - i) + 16)
                pe.wait_ge(xgT_ev, e + 1)
                wait(pe, hid_a, 2 * e)
                wait(pe, hid_v, 2 * e)
                for f in range(FC):
                    mm(bank[f][:, 0:SLOTS], w1_s[i][:, 128 * f:128 * (f + 1)], xgT[i][:], start=True, stop=True)\
                        .then_inc(up_d, 1)
                if more:
                    transpose_slots(e + 1, 1 - i)
                pe.wait_ge(w2_in[i], 8 * (e - i) + 16)
                wait(pe, obias_d, e - 1)
                for f in range(FC):
                    pe.wait_ge(hid_v if f % 2 else hid_a, 2 * e + 1 + f // 2)
                    for t in range(SLOT_TILES):
                        last = mm(bank[6 + i][0:SLOT_TILE, D * t:D * (t + 1)],
                                  hid[i][:, f, SLOT_TILE * t:SLOT_TILE * (t + 1)], w2_s[i][:, f, :],
                                  start=(f == 0 and t == 0), stop=(f == FC - 1), skip_group_check=True)
                last.then_inc(down_d, 1)

            transpose_slots(0, 0)
            expert(0, 0, True)
            expert(1, 1, True)
            with pe.Fori(1, E // 2 - 1) as two:
                expert(2 * two, 0, True)
                expert(2 * two + 1, 1, True)
            expert(E - 2, 0, True)
            expert(E - 1, 1, False)


def kernel(x, ctx_1024, mask_BxSxS2_bf1, L0_xattn_Wk, L0_xattn_bk, L0_xattn_Wq, L0_xattn_bq, L0_xattn_Wv,
           L0_xattn_bv, L0_xattn_Wo, L0_xattn_bo, L0_ffn_gate_w, L0_ffn_gate_b, L0_ffn_w1, L0_ffn_b1,
           L0_ffn_w2, L0_ffn_b2):
    import concourse.bacc as bacc
    from concourse.bass_utils import run_bass_kernel_spmd

    def by_feature(a):
        a = np.asarray(a)
        return np.ascontiguousarray(a.reshape(*a.shape[:-1], H, HD).swapaxes(-1, -2).reshape(a.shape))

    arrays = {
        "x": np.asarray(x), "ctx": np.asarray(ctx_1024), "mask": np.asarray(mask_BxSxS2_bf1).view(np.uint8),
        "wk": by_feature(L0_xattn_Wk), "bk": by_feature(L0_xattn_bk),
        "wq": by_feature(L0_xattn_Wq), "bq": by_feature(L0_xattn_bq),
        "wv": np.asarray(L0_xattn_Wv), "bv": np.asarray(L0_xattn_bv),
        "wo": np.asarray(L0_xattn_Wo), "bo": np.asarray(L0_xattn_bo),
        "gate_w": np.asarray(L0_ffn_gate_w), "gate_b": np.asarray(L0_ffn_gate_b),
        "w1": np.asarray(L0_ffn_w1),
        "b1": np.ascontiguousarray(np.asarray(L0_ffn_b1).reshape(E, FC, 128).transpose(2, 0, 1)),
        "w2": np.asarray(L0_ffn_w2), "b2": np.asarray(L0_ffn_b2),
    }
    nc = bacc.Bacc("TRN2", target_bir_lowering=False, num_devices=1)
    ins, feed = [], {}
    for name, a in arrays.items():
        a = np.ascontiguousarray(a)
        feed[f"{name}_in"] = a
        ins.append(nc.dram_tensor(f"{name}_in", a.shape, mybir.dt.from_np(a.dtype), kind="ExternalInput").ap())
    out = nc.dram_tensor("out", (B, S, D), mybir.dt.float32, kind="ExternalOutput").ap()
    build(nc, *ins, out)
    return run_bass_kernel_spmd(nc, [feed], core_ids=[0]).results[0]["out"]
```
